# Optimizing a Trainium2 kernel written in Bass

```python
import numpy as np
import jax
import jax.numpy as jnp

def _softmax(x, axis=-1):
    return jax.nn.softmax(x, axis=axis)

def _gelu(x):
    return jax.nn.gelu(x, approximate=True)

def _silu(x):
    return jax.nn.silu(x)

def _sigmoid(x):
    return jax.nn.sigmoid(x)

def _layernorm(x, axis=-1, eps=1e-05):
    m = jnp.mean(x, axis=axis, keepdims=True)
    v = jnp.var(x, axis=axis, keepdims=True)
    return (x - m) / jnp.sqrt(v + eps)

def _scatter_add(tgt, idx, src, axis=0):
    return tgt.at[idx].add(src)

def _segment_sum(src, seg, n):
    return jax.ops.segment_sum(src, seg, n)
kernel_name = 'mk_adaln_d1_jaxref_r8_06bfbe'

def setup_inputs(seed: int=0):
    np.random.seed(seed)
    _w = jnp.asarray

    def _L0_attn_setup():
        import jax, jax.numpy as jnp
        import numpy as np
        B, S, HID = (2, 256, 128)
        NH, NKV, D = (16, 4, 64)
        SCALE = 1.0 / np.sqrt(D).astype(np.float32)
        SOFTCAP = 30.0
        WINDOW = 128
        NEG = -1e+30
        key = jax.random.key(seed)
        kx, kq, kk, kv, ko = jax.random.split(key, 5)
        std = 0.02
        return {'x': jax.random.normal(kx, (B, S, HID), jnp.float32), 'Wq': jax.random.normal(kq, (NH * D, HID), jnp.float32) * std, 'Wk': jax.random.normal(kk, (NKV * D, HID), jnp.float32) * std, 'Wv': jax.random.normal(kv, (NKV * D, HID), jnp.float32) * std, 'Wo': jax.random.normal(ko, (HID, NH * D), jnp.float32) * std}
    _L0_attn_in = _L0_attn_setup()

    def _L0_ffn_setup():
        import jax, jax.numpy as jnp
        import numpy as np

        def _moe_forward(x, Wg, W1, b1, W2, b2):
            B, S, H = x.shape
            E = Wg.shape[1]
            tokens = x.reshape(-1, H)
            T = tokens.shape[0]
            C = -(-T // E)
            logits = tokens @ Wg
            gates = jax.nn.softmax(logits, axis=-1)
            idx = jnp.argmax(gates, axis=1)
            mask1 = jax.nn.one_hot(idx, E, dtype=gates.dtype)
            locations1 = jnp.cumsum(mask1, axis=0) - 1.0
            mask1 = mask1 * (locations1 < C).astype(gates.dtype)
            loc_s = jnp.sum(locations1 * mask1, axis=1).astype(jnp.int32)
            gates1 = jnp.sum(gates * mask1, axis=1)
            loc_oh = jax.nn.one_hot(loc_s, C, dtype=gates.dtype)
            dispatch = mask1[:, :, None] * loc_oh[:, None, :]
            combine = gates1[:, None, None] * dispatch
            expert_in = jnp.einsum('tec,th->ech', dispatch, tokens)
            hidden = jax.nn.relu(jnp.einsum('ech,ehf->ecf', expert_in, W1) + b1[:, None, :])
            expert_out = jnp.einsum('ecf,efh->ech', hidden, W2) + b2[:, None, :]
            out = jnp.einsum('tec,ech->th', combine, expert_out)
            return out.reshape(B, S, H)
        key = jax.random.key(seed)
        ks = jax.random.split(key, 6)
        B, S, H, F, E = (4, 256, 128, 512, 8)
        x = jax.random.normal(ks[0], (B, S, H), dtype=jnp.float32)
        Wg = jax.random.normal(ks[1], (H, E), dtype=jnp.float32) * (1.0 / np.sqrt(H))
        W1 = jax.random.normal(ks[2], (E, H, F), dtype=jnp.float32) * (1.0 / np.sqrt(H))
        b1 = jnp.zeros((E, F), dtype=jnp.float32)
        W2 = jax.random.normal(ks[3], (E, F, H), dtype=jnp.float32) * (1.0 / np.sqrt(F))
        b2 = jnp.zeros((E, H), dtype=jnp.float32)
        return {'x': x, 'Wg': Wg, 'W1': W1, 'b1': b1, 'W2': W2, 'b2': b2}
    _L0_ffn_in = _L0_ffn_setup()
    _L0_c = _w((lambda *s: np.random.randn(*s).astype(np.float32) * 0.05)(4, 128))
    _L0_wmod = _w((lambda *s: np.random.randn(*s).astype(np.float32) * 0.05)(128, 6 * 128) * 128 ** (-0.5))
    _d = {'L0_attn_x': _L0_attn_in['x'], 'L0_attn_Wq': _L0_attn_in['Wq'], 'L0_attn_Wk': _L0_attn_in['Wk'], 'L0_attn_Wv': _L0_attn_in['Wv'], 'L0_attn_Wo': _L0_attn_in['Wo'], 'L0_ffn_Wg': _L0_ffn_in['Wg'], 'L0_ffn_W1': _L0_ffn_in['W1'], 'L0_ffn_b1': _L0_ffn_in['b1'], 'L0_ffn_W2': _L0_ffn_in['W2'], 'L0_ffn_b2': _L0_ffn_in['b2'], 'L0_c': _L0_c, 'L0_wmod': _L0_wmod}
    _x0 = _d['L0_attn_x']
    _d['L0_attn_x'] = jax.random.normal(jax.random.fold_in(jax.random.key(seed), 1), (4, 1024, 128), dtype=_x0.dtype)
    del _x0
    return _d

def reference(L0_attn_x, L0_attn_Wq, L0_attn_Wk, L0_attn_Wv, L0_attn_Wo, L0_ffn_Wg, L0_ffn_W1, L0_ffn_b1, L0_ffn_W2, L0_ffn_b2, L0_c, L0_wmod):

    def _L0_attn_ref(x, Wq, Wk, Wv, Wo):
        import jax, jax.numpy as jnp
        import numpy as np
        B, S, HID = (2, 256, 128)
        NH, NKV, D = (16, 4, 64)
        SCALE = 1.0 / np.sqrt(D).astype(np.float32)
        SOFTCAP = 30.0
        WINDOW = 128
        NEG = -1e+30
        b, s, _ = x.shape
        n_rep = NH // NKV
        q = (x @ Wq.T).reshape(b, s, NH, D)
        k = (x @ Wk.T).reshape(b, s, NKV, D)
        v = (x @ Wv.T).reshape(b, s, NKV, D)
        k = jnp.repeat(k, n_rep, axis=2)
        v = jnp.repeat(v, n_rep, axis=2)
        scores = jnp.einsum('bqhd,bkhd->bhqk', q, k) * SCALE
        scores = SOFTCAP * jnp.tanh(scores / SOFTCAP)
        i = jnp.arange(s)[:, None]
        j = jnp.arange(s)[None, :]
        mask = (j <= i) & (j > i - WINDOW)
        scores = jnp.where(mask, scores, NEG)
        p = jax.nn.softmax(scores, axis=-1)
        o = jnp.einsum('bhqk,bkhd->bqhd', p, v).reshape(b, s, NH * D)
        return o @ Wo.T

    def _L0_ffn_ref(x, Wg, W1, b1, W2, b2):
        import jax, jax.numpy as jnp
        import numpy as np

        def _moe_forward(x, Wg, W1, b1, W2, b2):
            B, S, H = x.shape
            E = Wg.shape[1]
            tokens = x.reshape(-1, H)
            T = tokens.shape[0]
            C = -(-T // E)
            logits = tokens @ Wg
            gates = jax.nn.softmax(logits, axis=-1)
            idx = jnp.argmax(gates, axis=1)
            mask1 = jax.nn.one_hot(idx, E, dtype=gates.dtype)
            locations1 = jnp.cumsum(mask1, axis=0) - 1.0
            mask1 = mask1 * (locations1 < C).astype(gates.dtype)
            loc_s = jnp.sum(locations1 * mask1, axis=1).astype(jnp.int32)
            gates1 = jnp.sum(gates * mask1, axis=1)
            loc_oh = jax.nn.one_hot(loc_s, C, dtype=gates.dtype)
            dispatch = mask1[:, :, None] * loc_oh[:, None, :]
            combine = gates1[:, None, None] * dispatch
            expert_in = jnp.einsum('tec,th->ech', dispatch, tokens)
            hidden = jax.nn.relu(jnp.einsum('ech,ehf->ecf', expert_in, W1) + b1[:, None, :])
            expert_out = jnp.einsum('ecf,efh->ech', hidden, W2) + b2[:, None, :]
            out = jnp.einsum('tec,ech->th', combine, expert_out)
            return out.reshape(B, S, H)
        return _moe_forward(x, Wg, W1, b1, W2, b2)
    x = L0_attn_x
    mod = (_silu(L0_c) @ L0_wmod).reshape(L0_c.shape[0], 6, 1, -1)
    sa, ca, ga, sb, cb, gb = (mod[:, 0], mod[:, 1], mod[:, 2], mod[:, 3], mod[:, 4], mod[:, 5])
    ga = (2 * (ga >= 0) - 1) * jnp.maximum(jnp.abs(ga), 0.25)
    gb = (2 * (gb >= 0) - 1) * jnp.maximum(jnp.abs(gb), 0.25)
    h = _layernorm(x, axis=-1) * (1 + ca) + sa
    x = x + ga * _L0_attn_ref(h, L0_attn_Wq, L0_attn_Wk, L0_attn_Wv, L0_attn_Wo)
    h = _layernorm(x, axis=-1) * (1 + cb) + sb
    x = x + gb * _L0_ffn_ref(h, L0_ffn_Wg, L0_ffn_W1, L0_ffn_b1, L0_ffn_W2, L0_ffn_b2)
    return x

_drawn_inputs = setup_inputs


def setup_inputs(seed=0):
    import zlib

    import numpy as np

    out = dict(_drawn_inputs(seed))
    spreads = {'L0_ffn_b1': (0.0, 0.8), 'L0_ffn_b2': (0.0, 0.8)}
    factors = {'L0_attn_Wq': 8.0, 'L0_attn_Wk': 8.0, 'L0_attn_Wv': 8.0, 'L0_attn_Wo': 8.0}
    for name, (base, spread) in spreads.items():
        noise = np.random.default_rng([zlib.crc32(name.encode()), seed]).standard_normal(out[name].shape)
        drawn = base * np.exp(spread * noise) if base else spread * noise
        out[name] = jnp.asarray(drawn.astype(out[name].dtype))
    for name, factor in factors.items():
        out[name] = (out[name] * factor).astype(out[name].dtype)
    return out
```

```python
from contextlib import ExitStack

import numpy as np

import concourse.bass as bass
from concourse import mybir

F32 = mybir.dt.float32
F32R = mybir.dt.float32r
BF16 = mybir.dt.bfloat16
I32 = mybir.dt.int32
U32 = mybir.dt.uint32
ALU = mybir.AluOpType
ACT = mybir.ActivationFunctionType

P = 128
BATCHES = 4
SEQ = 1024
HEADS, KV, D = 16, 4, 64
REP = HEADS // KV
SOFTCAP = 30.0
SCORE_SCALE = 1.0 / (D ** 0.5 * SOFTCAP)
EPS = 1e-5
EXPERTS, FF = 8, 512
FC = FF // P
TOKENS = BATCHES * SEQ
TILES = TOKENS // P
BATCH_TILES = SEQ // P
BLOCKS = TILES // 2
BT = 2 * P
CAP = TOKENS // EXPERTS
ST = CAP // P
HALF = P // 2

ROW_H, ROW_G, ROW_X, ROW_ID, ROW = 0, P, 2 * P, 3 * P, 400
NO_TOKEN = 1 << 20

TURNS = 6
K_RING, T_RING, V_RING, VD_RING, P_RING, PM_RING, PAY_RING = 3, 2, 6, 4, 4, 3, 3


class Signal:

    def __init__(self, sem, unit=1):
        self.sem, self.unit, self.count, self.at = sem, unit, 0, {}

    def next(self, key):
        self.count += self.unit
        self.at[key] = self.count


class Queue:

    def __init__(self):
        self.items, self.passed = [], {}

    def step(self, waits, emit, signal=None, key=None):
        needed = []
        for s, k in waits:
            value = s.at[k]
            if self.passed.get(id(s), 0) < value:
                self.passed[id(s)] = value
                needed.append((s.sem, value))
        if signal is not None:
            signal.next(key)
        self.items.append((needed, emit, signal))

    def run(self, engine):
        for needed, emit, signal in self.items:
            for sem, value in needed:
                engine.wait_ge(sem, value)
            last = emit(engine)
            if signal is not None:
                last.then_inc(signal.sem, signal.unit)


def build(nc, x, wq, wk, wv, wo, wg, w1, b1, w2, b2, c, wmod, out):
    sorted_rows = nc.dram_tensor("sorted_rows", [TOKENS, ROW], F32, kind="Internal").ap()
    ctx = ExitStack()
    with ctx:
        def sb(name, shape, dt=F32):
            return ctx.enter_context(nc.sbuf_tensor(name, shape, dt))

        def pb(name, shape):
            return ctx.enter_context(nc.psum_tensor(name, shape, F32))

        def signal(name, unit=1):
            return Signal(ctx.enter_context(nc.semaphore(name)), unit)

        x_sb = sb("x_sb", [P, TILES, P])
        T = sb("T", [P, T_RING, HEADS, BT], F32R)
        KH = sb("KH", [P, K_RING, KV, BT], F32R)
        KL = sb("KL", [P, K_RING, KV, BT], F32R)
        V = sb("V", [P, V_RING, KV * D])
        VD = sb("VD", [P, VD_RING, KV * D])
        PR = sb("PR", [P, P_RING, 2 * REP * P])
        PM = sb("PM", [P, PM_RING, 2 * REP * P])
        OU = sb("OU", [P, 4, REP * P])
        ON = sb("ON", [P, 2, REP * P])
        SUMS = sb("SUMS", [P, REP * P])
        RS = sb("RS", [P, HEADS])
        RX = sb("RX", [P, HEADS, D])
        w_stage = sb("w_stage", [P, EXPERTS * FF])
        WqH, WqL = sb("WqH", [P, HEADS * D], F32R), sb("WqL", [P, HEADS * D], F32R)
        WkH, WkL = sb("WkH", [P, KV, 2, D], F32R), sb("WkL", [P, KV, 2, D], F32R)
        WvH, WvL = sb("WvH", [P, KV * D], F32R), sb("WvL", [P, KV * D], F32R)
        Wo = sb("Wo", [P, 2 * REP, P])
        Wg = sb("Wg", [P, EXPERTS])
        W2 = sb("W2", [P, EXPERTS, FC, P])
        b1_col = sb("b1_col", [P, EXPERTS, FC])
        cT = sb("cT", [P, BATCHES])
        c_e = sb("c_e", [P, BATCHES])
        c_r = sb("c_r", [P, BATCHES])
        siluT = sb("siluT", [P, BATCHES])
        sa_col = sb("sa_col", [P, BATCHES])
        ca_col = sb("ca_col", [P, BATCHES])
        mod = sb("mod", [P, BATCHES, 4, P])
        XN = sb("XN", [P, BT])
        XF = sb("XF", [P, BT])
        XH, XL = sb("XH", [P, 2, BT], F32R), sb("XL", [P, 2, BT], F32R)
        stats1, mv1 = sb("stats1", [P, 2, 6]), sb("mv1", [P, TILES, 2])
        stats2, mv2 = sb("stats2", [P, 6]), sb("mv2", [P, TILES, 2])
        var1, rstd1 = sb("var1", [P, TILES]), sb("rstd1", [P, TILES])
        var2, rstd2 = sb("var2", [P, TILES]), sb("rstd2", [P, TILES])
        PAY = sb("PAY", [P, PAY_RING, ROW])
        h2T = sb("h2T", [P, P])
        logits, e8 = sb("logits", [P, TILES, 8]), sb("e8", [P, 8])
        top, top_at = sb("top", [P, TILES, 8]), sb("top_at", [P, TILES, 8], U32)
        neg_top, e_sum, gate = sb("neg_top", [P, TILES]), sb("e_sum", [P, TILES]), sb("gate", [P, TILES])
        onehot = sb("onehot", [P, TILES, EXPERTS], BF16)
        seen = sb("seen", [P, TILES + 1, EXPERTS], BF16)
        prod8 = sb("prod8", [P, EXPERTS])
        loc, slot, over = sb("loc", [P, TILES]), sb("slot", [P, TILES]), sb("over", [P, TILES])
        slot_i = sb("slot_i", [P, TILES], I32)
        zeros = sb("zeros", [P, P])
        ident = sb("ident", [P, P])
        before = sb("before", [P, P])
        earlier = ON[:, 1, 0:P]
        earlier_b = sb("earlier_b", [P, P], BF16)
        ones_b = sb("ones_b", [P, P], BF16)
        ones32 = sb("ones32", [P, 32])
        neg_half = sb("neg_half", [P, 2])
        iota8i, iota8 = sb("iota8i", [P, EXPERTS], I32), sb("iota8", [P, EXPERTS])
        tok_id = sb("tok_id", [P, TILES], I32)
        empty_row = PAY[:, PAY_RING - 1, :]
        rows = []
        for wide in (x_sb[:, :, :].rearrange("p a b -> p (a b)"), T[:, :, :, :].rearrange("p a b c -> p (a b c)").bitcast(F32),
                     KH[:, :, :, :].rearrange("p a b c -> p (a b c)").bitcast(F32)):
            for i in range(wide.shape[1] // (ST * ROW)):
                rows.append(wide[:, i * ST * ROW:(i + 1) * ST * ROW].rearrange("p (s r) -> p s r", r=ROW))
        w1_sb = w_stage[:, :].rearrange("p (e f) -> p e f", e=EXPERTS)
        hidden = [PR[:, 2 * n:2 * n + 2, :].rearrange("p a (b s) -> p (a b) s", s=CAP) for n in range(2)]
        xT = OU
        b2_row = V[:, 0:4, :].rearrange("p a (b n) -> p (a b) n", n=P)
        done_rows = [PM[:, n, 0:ST * P].rearrange("p (s d) -> p s d", s=ST) for n in range(2)]

        own = pb("own", [P, 2, REP * P])
        turns = pb("turns", [P, TURNS, 512])

        x_in = [signal(f"x_in{b}", 16) for b in range(BATCHES)]
        w_in = {n: signal(f"{n}_in", 16) for n in ("wk", "wq", "wv", "c", "wmod", "wo", "w1", "b2", "rest")}
        empty_in = signal("empty_in", 16)
        pay_out = [signal(f"pay_out{n}", 16) for n in range(PAY_RING)]
        x1_out = [signal(f"x1_out{n}", 16) for n in range(PAY_RING)]
        rows_in = [signal(f"rows_in{n}", 16) for n in range(EXPERTS)]
        final_out = [signal(f"final_out{n}", 16) for n in range(2)]
        consts, consts_v = signal("consts"), signal("consts_v")
        prep_a, prep_v, prep_t = signal("prep_a"), signal("prep_v"), signal("prep_t")
        split_h, split_l = signal("split_h"), signal("split_l")
        ln1_v, ln1_p, normed1 = signal("ln1_v"), signal("ln1_p"), signal("normed1")
        x_turned, xh_done, xf_done, xl_done = (signal(n) for n in ("x_turned", "xh_done", "xf_done", "xl_done"))
        projected, h_kept, l_kept = signal("projected"), signal("h_kept"), signal("l_kept")
        v_kept, vd_done = signal("v_kept"), signal("vd_done")
        scored, merged, tanhed, exped, masked = (signal(n) for n in ("scored", "merged", "tanhed", "exped", "masked"))
        pv_done, o_kept, summed, sums_kept = (signal(n) for n in ("pv_done", "o_kept", "summed", "sums_kept"))
        sums_turned, inverted, repeated, rs_turned = (signal(n) for n in ("sums_turned", "inverted", "repeated", "rs_turned"))
        scaled, wo_done, tail_v, ln2_p, payload_p = (signal(n) for n in ("scaled", "wo_done", "tail_v", "ln2_p", "payload_p"))
        h2_turned, h2_kept, logits_done, gate_e, placed = (signal(n) for n in ("h2_turned", "h2_kept", "logits_done", "gate_e", "placed"))
        route_v = signal("route_v")
        rows_turned, xT_kept, up_done, relu_done, down_done, out_v = (
            signal(n) for n in ("rows_turned", "xT_kept", "up_done", "relu_done", "down_done", "out_v"))

        sp, pe, act, dve, pool = Queue(), Queue(), Queue(), Queue(), Queue()

        class Banks:
            turn, readers = 0, [[] for _ in range(TURNS)]

            def take(self):
                n = self.turn
                self.turn = (n + 1) % TURNS
                return n, turns[:, n, :], list(self.readers[n])

            def read_by(self, n, *who):
                self.readers[n] = list(who)

        banks = Banks()

        x_v = x.rearrange("(b t p) d -> b p t d", t=BATCH_TILES, p=P)

        def load(dst, src, s, key="in"):
            sp.step([], lambda e: e.dma_start(dst, src), s, key)

        stage_q = w_stage[:, 0:HEADS * D]
        stage_k = w_stage[:, 1024:1024 + 2 * KV * D].rearrange("p (g a d) -> p g a d", g=KV, a=2)
        stage_v = w_stage[:, 2048:2048 + KV * D]
        stage_m = w_stage[:, 3072:3072 + 6 * P]
        load(x_sb[:, 0:BATCH_TILES, :], x_v[0], x_in[0])
        load(cT[:, :], c, w_in["c"])
        load(stage_m, wmod, w_in["wmod"])
        for a in range(2):
            load(stage_k[:, :, a, :], wk.rearrange("p (g d) -> p g d", g=KV), w_in["wk"], a)
        load(stage_v, wv, w_in["wv"])
        load(stage_q, wq, w_in["wq"])
        for b in range(1, BATCHES):
            load(x_sb[:, b * BATCH_TILES:(b + 1) * BATCH_TILES, :], x_v[b], x_in[b])
        wo_v = wo.rearrange("(p h r d) n -> h d p r n", p=2, h=2, r=REP)
        for h in range(2):
            for p in range(2):
                load(Wo[h * HALF:(h + 1) * HALF, p * REP:(p + 1) * REP, :], wo_v[h, :, p], w_in["wo"], (h, p))
        load(Wg[:, :], wg, w_in["rest"], 0)
        load(b1_col[:, :, :], b1, w_in["rest"], 1)
        load(W2[:, :, :, :].rearrange("p e c n -> p (e c) n"), w2.rearrange("e (c p) n -> p (e c) n", p=P),
             w_in["rest"], 3)

        def const(emit, key, waits=()):
            pool.step([(consts, k) for k in waits], emit, consts, key)

        const(lambda e: e.memset(zeros[:, :], 0.0), "zeros")
        const(lambda e: e.memset(ones32[:, :], 1.0), "ones32")
        const(lambda e: e.memset(ones_b[:, :], 1.0), "ones_b")
        const(lambda e: e.memset(neg_half[:, :], -0.5), "neg_half")
        const(lambda e: e.memset(seen[:, 0, :], 0.0), "seen")
        const(lambda e: e.memset(PAY[:, :, :], 0.0), "empty0")
        const(lambda e: e.affine_select(out=ident[:, :], in_=zeros[:, :], compare_op=ALU.not_equal, fill=1.0,
                                        base=0, pattern=[[-1, P]], channel_multiplier=1), "ident", ["zeros"])
        const(lambda e: e.affine_select(out=before[:, :], in_=zeros[:, :], compare_op=ALU.is_ge, fill=1.0,
                                        base=0, pattern=[[1, P]], channel_multiplier=-1), "before")
        const(lambda e: e.affine_select(out=earlier, in_=zeros[:, :], compare_op=ALU.is_ge, fill=1.0,
                                        base=0, pattern=[[-1, P]], channel_multiplier=1), "earlier")
        const(lambda e: e.memset(empty_row[:, ROW_ID:ROW_ID + 1].bitcast(I32), NO_TOKEN), "empty", ["empty0"])
        const(lambda e: e.iota(iota8i[:, :], pattern=[[1, EXPERTS]], base=0, channel_multiplier=0), "iota8i")
        const(lambda e: e.iota(tok_id[:, :], pattern=[[P, TILES]], base=0, channel_multiplier=1), "tok_id")
        const(lambda e: e.tensor_copy(iota8[:, :], iota8i[:, :]), "iota8", ["iota8i"])
        const(lambda e: e.tensor_copy(earlier_b[:, :], earlier), "earlier_b", ["earlier"])
        all_consts = (consts, "earlier_b")

        sp.step([all_consts],
                lambda e: e.dma_start(sorted_rows.rearrange("(n p) r -> p n r", p=P),
                                      empty_row.unsqueeze(1).to_broadcast([P, TILES, ROW])), empty_in, "all")

        act.step([(w_in["c"], "in")], lambda e: e.activation(c_e[:, :], cT[:, :], ACT.Exp, scale=-1.0), prep_a, "exp")
        dve.step([(prep_a, "exp")], lambda e: e.tensor_scalar(c_e[:, :], c_e[:, :], 1.0, None, ALU.add), prep_v, "1+e")
        dve.step([(prep_v, "1+e")], lambda e: e.reciprocal(c_r[:, :], c_e[:, :]), prep_v, "r")
        dve.step([(prep_v, "r")], lambda e: e.tensor_tensor(siluT[:, :], cT[:, :], c_r[:, :], ALU.mult), prep_v, "silu")

        n, mod_ps, _ = banks.take()

        def mod_columns(e):
            for j in range(2):
                last = e.matmul(mod_ps[:, 4 * j:4 * j + BATCHES], stage_m[:, j * P:(j + 1) * P], siluT[:, :],
                                start=True, stop=True)
            return last
        pe.step([(prep_v, "silu"), (w_in["wmod"], "in")], mod_columns, prep_t, "columns")
        dve.step([(prep_t, "columns")], lambda e: e.tensor_copy(sa_col[:, :], mod_ps[:, 0:BATCHES]), prep_v, "sa")
        dve.step([], lambda e: e.tensor_scalar(ca_col[:, :], mod_ps[:, 4:4 + BATCHES], 1.0, None, ALU.add), prep_v, "ca")
        banks.read_by(n, (prep_v, "ca"))
        for b in range(BATCHES):
            n, ps, free = banks.take()
            pe.step(free, lambda e, b=b, ps=ps: e.matmul(ps, siluT[:, b:b + 1].to_broadcast([P, P]),
                                                stage_m[:, 2 * P:6 * P], start=True, stop=True), prep_t, b)
            act.step([(prep_t, b)], lambda e, b=b, ps=ps: e.activation(
                mod[:, b, :, :].rearrange("p j n -> p (j n)"), ps, ACT.Copy), prep_a, b)
            banks.read_by(n, (prep_a, b))

        def split(H, L, src, key, waits):
            act.step(waits, lambda e: e.activation(H, src, ACT.Copy), split_h, key)
            dve.step([(split_h, key)], lambda e: e.tensor_tensor(L, src, H.bitcast(F32), ALU.subtract), split_l, key)

        split(WkH[:, :, :, :].rearrange("p g a d -> p (g a d)"), WkL[:, :, :, :].rearrange("p g a d -> p (g a d)"),
              w_stage[:, 1024:1024 + 2 * KV * D], "wk", [(w_in["wk"], 1)])

        def finish_modulation():
            dve.step([(prep_a, BATCHES - 1)],
                     lambda e: e.tensor_scalar(mod[:, :, 2, :], mod[:, :, 2, :], 1.0, None, ALU.add), prep_v, "cb")
            for j in (0, 3):
                sign = PM[:, 0, 0:BATCHES * P].rearrange("p (b n) -> p b n", b=BATCHES)
                size = PM[:, 1, 0:BATCHES * P].rearrange("p (b n) -> p b n", b=BATCHES)
                g = mod[:, :, j, :]
                dve.step([(prep_v, ("gate", 0))] if j else [], lambda e, g=g, sign=sign: e.tensor_scalar(
                    sign, g, 0.0, 0.5, ALU.is_ge, ALU.subtract), prep_v, ("sign", j))
                dve.step([], lambda e, g=g, size=size: e.scalar_tensor_tensor(
                    size, g, -1.0, g, ALU.mult, ALU.max), prep_v, ("size", j))
                dve.step([(prep_v, ("size", j))], lambda e, sign=sign, size=size: e.scalar_tensor_tensor(
                    size, size, 0.25, sign, ALU.max, ALU.mult), prep_v, ("half", j))
                dve.step([(prep_v, ("half", j))], lambda e, g=g, size=size: e.tensor_scalar(
                    g, size, 2.0, None, ALU.mult), prep_v, ("gate", j))

        def ln1(k):
            tiles = (2 * k, 2 * k + 1)
            for t in tiles:
                dve.step([(x_in[t // BATCH_TILES], "in")] + ([(ln1_v, ("mv", t - 2))] if t >= 2 else []),
                         lambda e, t=t: e.bn_stats(stats1[:, t % 2, :], x_sb[:, t, :]), ln1_v, ("stats", t))
            for t in tiles:
                dve.step([(ln1_v, ("stats", t))],
                         lambda e, t=t: e.bn_aggr(mv1[:, t, :], stats1[:, t % 2, :]), ln1_v, ("mv", t))
            s = slice(2 * k, 2 * k + 2)
            pool.step([(ln1_v, ("mv", tiles[1]))], lambda e: e.tensor_scalar(
                var1[:, s], mv1[:, s, 1], EPS, 1.0, ALU.add, ALU.mult), ln1_p, ("var", k))
            pool.step([(ln1_p, ("var", k))], lambda e: e.tensor_tensor(
                rstd1[:, s], var1[:, s], neg_half[:, :], ALU.pow), ln1_p, ("rstd", k))

        def normalise1(k):
            for j, t in enumerate((2 * k, 2 * k + 1)):
                dve.step([(ln1_p, ("rstd", k))] + ([(x_turned, k - 1)] if k else []),
                         lambda e, t=t, j=j: e.tensor_scalar(
                             XN[:, j * P:(j + 1) * P], x_sb[:, t, :], mv1[:, t, 0:1], rstd1[:, t:t + 1],
                             ALU.subtract, ALU.mult), normed1, t)

        def turn_x(k):
            b = 2 * k // BATCH_TILES
            n, ps, free = banks.take()

            def turn(e):
                for j in range(2):
                    last = e.transpose(ps[:, j * P:(j + 1) * P], XN[:, j * P:(j + 1) * P], ident[:, :])
                return last
            pe.step([(normed1, 2 * k + 1), all_consts] + free, turn, x_turned, k)
            used = [(projected, ("v", k - 2))] if k >= 2 else []
            act.step([(x_turned, k), (prep_v, "ca")] + used, lambda e: e.activation(
                XH[:, k % 2, :], ps[:, 0:BT], ACT.Identity, bias=sa_col[:, b:b + 1], scale=ca_col[:, b:b + 1]),
                xh_done, k)
            dve.step([(xh_done, k)] + ([(xl_done, k - 1)] if k else []), lambda e: e.tensor_scalar(
                XF[:, :], ps[:, 0:BT], ca_col[:, b:b + 1], sa_col[:, b:b + 1], ALU.mult, ALU.add), xf_done, k)
            dve.step([(xf_done, k)] + used, lambda e: e.tensor_tensor(
                XL[:, k % 2, :], XF[:, :], XH[:, k % 2, :].bitcast(F32), ALU.subtract), xl_done, k)
            banks.read_by(n, (xf_done, k))

        def three_passes(e, dst, wh, wl, xh, xl):
            e.matmul(dst, wh, xh, start=True, stop=False)
            e.matmul(dst, wh, xl, start=False, stop=False)
            return e.matmul(dst, wl, xh, start=False, stop=True)

        def project_k(k, i):
            n, ps, free = banks.take()
            ps = ps.rearrange("p (g n) -> p g n", g=2)

            def mm(e):
                for a in range(2):
                    last = three_passes(e, ps[:, a, :], WkH[:, 2 * i + a, :, :].rearrange("p a d -> p (a d)"),
                                        WkL[:, 2 * i + a, :, :].rearrange("p a d -> p (a d)"),
                                        XH[:, k % 2, :], XL[:, k % 2, :])
                return last
            pe.step([(xl_done, k), (split_l, "wk")] + free, mm, projected, ("k", k, i))
            used = [(scored, (2 * k - 4, 1))] if k >= 3 else []
            kh, kl = KH[:, k % K_RING, 2 * i:2 * i + 2, :], KL[:, k % K_RING, 2 * i:2 * i + 2, :]
            act.step([(projected, ("k", k, i))] + used, lambda e: e.activation(kh, ps, ACT.Copy), h_kept, ("k", k, i))
            dve.step([(h_kept, ("k", k, i))], lambda e: e.tensor_tensor(kl, ps, kh.bitcast(F32), ALU.subtract),
                     l_kept, ("k", k, i))
            banks.read_by(n, (l_kept, ("k", k, i)))

        def project_v(k):
            n, ps, free = banks.take()

            def mm(e):
                for j in range(2):
                    tok = slice(j * P, (j + 1) * P)
                    dst = ps[:, j * BT:(j + 1) * BT]
                    e.matmul(dst, XH[:, k % 2, tok], WvH[:, :], start=True, stop=False)
                    e.matmul(dst, XL[:, k % 2, tok], WvH[:, :], start=False, stop=False)
                    last = e.matmul(dst, XH[:, k % 2, tok], WvL[:, :], start=False, stop=True)
                return last
            pe.step([(xl_done, k), (split_l, "wv")] + free, mm, projected, ("v", k))
            used = [(pv_done, (2 * k - 4, 1))] if k >= 3 else []
            r = 2 * k % V_RING
            act.step([(projected, ("v", k))] + used, lambda e: e.activation(
                V[:, r:r + 2, :], ps.rearrange("p (t n) -> p t n", t=2), ACT.Copy), v_kept, k)
            banks.read_by(n, (v_kept, k))
            for t in (2 * k, 2 * k + 1):
                if t % BATCH_TILES:
                    used = [(pv_done, (t - VD_RING, 1))] if t >= VD_RING else []
                    pool.step([(v_kept, k)] + used, lambda e, t=t: e.tensor_tensor(
                        VD[:, t % VD_RING, :], V[:, t % V_RING, :], V[:, (t - 1) % V_RING, :], ALU.subtract),
                        vd_done, t)

        def project_q(k, g):
            n, ps, free = banks.take()
            ps = ps.rearrange("p (c n) -> p c n", c=2)

            def mm(e):
                for a in range(2):
                    w = slice((2 * g + a) * P, (2 * g + a + 1) * P)
                    last = three_passes(e, ps[:, a, :], WqH[:, w], WqL[:, w], XH[:, k % 2, :], XL[:, k % 2, :])
                return last
            pe.step([(xl_done, k), (split_l, "wq")] + free, mm, projected, ("q", k, g))
            used = [(scored, (2 * k - 3, 1))] if k >= 2 else []
            halves = (slice(0, HALF), slice(HALF, P))
            for odd in range(2):
                mine = halves[odd]
                act.step([(projected, ("q", k, g))] + used, lambda e, odd=odd, mine=mine: e.activation(
                    T[mine, k % T_RING, 4 * g + odd:4 * g + 4:2, :], ps[mine, :, :], ACT.Copy),
                    h_kept, ("q", k, g, odd))
            for odd in range(2):
                mine, other = halves[odd], halves[1 - odd]
                dve.step([(h_kept, ("q", k, g, odd))] + used, lambda e, odd=odd, mine=mine, other=other: e.tensor_tensor(
                    T[other, k % T_RING, 4 * g + odd:4 * g + 4:2, :], ps[mine, :, :],
                    T[mine, k % T_RING, 4 * g + odd:4 * g + 4:2, :].bitcast(F32), ALU.subtract),
                    l_kept, ("q", k, g, odd))
            banks.read_by(n, (l_kept, ("q", k, g, 1)))

        units = {}

        def scores(t, h):
            k, first = t // 2, t % BATCH_TILES == 0
            u = units[t, h] = 2 * t + h
            last_unit = (t, 0) if h else (t - 1, 1)

            def pair(e, dst, key_tile, g):
                q = T[:, k % T_RING, 4 * g:4 * g + 4, (t % 2) * P:(t % 2 + 1) * P]
                at = slice(key_tile % 2 * P, (key_tile % 2 + 1) * P)
                e.matmul(dst, KH[:, key_tile // 2 % K_RING, g, at], q, start=True, stop=False)
                return e.matmul(dst, KL[:, key_tile // 2 % K_RING, g, at], q, start=False, stop=True)

            for a in range(2):
                g = 2 * h + a
                pe.step([(l_kept, ("k", k, h)), (l_kept, ("q", k, g, 1))] + ([(tanhed, last_unit)] if u else []),
                        lambda e, a=a, g=g: pair(e, own[:, a, :], t, g), scored, (t, h, a))
            if first:
                source = (scored, (t, h, 1))
            else:
                for a in range(2):
                    g = 2 * h + a
                    n, ps, free = banks.take()
                    pe.step(free, lambda e, g=g, ps=ps: pair(e, ps, t - 1, g), scored, (t, h, "before", a))
                    dve.step([(scored, (t, h, "before", a))], lambda e, a=a, ps=ps: e.copy_predicated(
                        own[:, a, :].rearrange("p (r n) -> p r n", n=P),
                        before[:, :].bitcast(U32).unsqueeze(1).to_broadcast([P, REP, P]),
                        ps.rearrange("p (r n) -> p r n", n=P)), merged, (t, h, a))
                    banks.read_by(n, (merged, (t, h, a)))
                source = (merged, (t, h, 1))
            scored.at[t, h] = scored.count
            pr, pm = PR[:, u % P_RING, :], PM[:, u % PM_RING, :]
            used = [(summed, t - 2), (masked, (t - 2, h))] if t >= 2 else []
            act.step([source] + used, lambda e: e.activation(
                pr, own[:, :, :].rearrange("p a n -> p (a n)"), ACT.Tanh, scale=SCORE_SCALE), tanhed, (t, h))
            act.step([(tanhed, (t, h))], lambda e: e.activation(pr, pr, ACT.Exp, scale=SOFTCAP), exped, (t, h))
            used = []
            if u >= PM_RING:
                ot = (u - PM_RING) // 2
                used = [(pv_done, (ot, (u - PM_RING) % 2))]
                if ot % BATCH_TILES == 0:
                    used.append((summed, ot))
            pool.step([(exped, (t, h))] + used + ([(prep_v, ("gate", 3))] if u < 2 else []), lambda e: e.affine_select(
                out=pm.rearrange("p (r n) -> p r n", n=P), in_=pr.rearrange("p (r n) -> p r n", n=P),
                compare_op=ALU.is_ge, fill=0.0, base=0, pattern=[[0, 2 * REP], [1, P]], channel_multiplier=-1),
                masked, (t, h))

        def attend(t, h):
            first, u = t % BATCH_TILES == 0, units[t, h]
            n, ps, free = banks.take()

            def mm(e):
                parts = [(VD if not first else V, PM, u % PM_RING, (t % VD_RING if not first else t % V_RING))]
                if not first:
                    parts.insert(0, (V, PR, u % P_RING, (t - 1) % V_RING))
                for m, (v, p, pr, vr) in enumerate(parts):
                    for a in range(2):
                        g = 2 * h + a
                        last = e.matmul(ps[a * HALF:(a + 1) * HALF, :], v[:, vr, g * D:(g + 1) * D],
                                        p[:, pr, a * REP * P:(a + 1) * REP * P],
                                        start=(m == 0), stop=(m == len(parts) - 1))
                return last
            ready = [(masked, (t, h)), (v_kept, t // 2)] + ([] if first else [(vd_done, t)])
            pe.step(ready + free, mm, pv_done, (t, h))
            act.step([(pv_done, (t, h))] + ([(scaled, (t - 2, h))] if t >= 2 else []),
                     lambda e: e.activation(OU[:, u % 4, :], ps, ACT.Copy), o_kept, (t, h))
            banks.read_by(n, (o_kept, (t, h)))

        def sums(t):
            first = t % BATCH_TILES == 0
            n, ps, free = banks.take()

            def mm(e):
                for g in range(KV):
                    u = units[t, g // 2]
                    p = PM[:, u % PM_RING, :] if first else PR[:, u % P_RING, :]
                    last = e.matmul(ps[32 * g:32 * g + 32, :], ones32[:, :],
                                    p[:, (g % 2) * REP * P:(g % 2 + 1) * REP * P], start=True, stop=True,
                                    tile_position=(0, 32 * g))
                return last
            pe.step([(masked if first else exped, (t, 1))] + free, mm, summed, t)
            act.step([(summed, t)] + ([(sums_turned, t - 1)] if t else []),
                     lambda e: e.activation(SUMS[:, :], ps, ACT.Copy), sums_kept, t)
            banks.read_by(n, (sums_kept, t))

        def invert(t):
            n, ps, free = banks.take()

            def turn(e):
                for r in range(REP):
                    last = e.transpose(ps[:, r * P:(r + 1) * P], SUMS[:, r * P:(r + 1) * P], ident[:, :])
                return last
            pe.step([(sums_kept, t)] + free, turn, sums_turned, t)
            dve.step([(sums_turned, t)] + ([(repeated, t - 1)] if t else []), lambda e: e.reciprocal(
                RS[:, :].rearrange("q (p r h) -> q r p h", p=2, r=REP),
                ps[:, 0:REP * P:32].rearrange("q (r p h) -> q r p h", r=REP, p=2)), inverted, t)
            banks.read_by(n, (inverted, t))
            pool.step([(inverted, t)] + ([(rs_turned, (t - 1, 1))] if t else []), lambda e: e.tensor_scalar(
                RX[:, :, :], RS[:, :].unsqueeze(2).to_broadcast([P, HEADS, D]), 1.0, 1.0, ALU.mult, ALU.mult),
                repeated, t)

        def scale(t, h):
            n, ps, free = banks.take()

            def turn(e):
                for r in range(REP):
                    i = 2 * (h * REP + r)
                    last = e.transpose(ps[:, r * P:(r + 1) * P], RX[:, i:i + 2, :].rearrange("q a d -> q (a d)"), ident[:, :])
                return last
            pe.step([(repeated, t)] + free, turn, rs_turned, (t, h))
            dve.step([(rs_turned, (t, h)), (o_kept, (t, h))] + ([(wo_done, t - 1)] if t else []),
                     lambda e: e.tensor_tensor(ON[:, h, :], ps, OU[:, units[t, h] % 4, :], ALU.mult), scaled, (t, h))
            banks.read_by(n, (scaled, (t, h)))

        def out_project(t):
            b = t // BATCH_TILES
            n, ps, free = banks.take()

            def mm(e):
                for i in range(2 * REP):
                    last = e.matmul(ps[:, 0:P], ON[:, i // REP, (i % REP) * P:(i % REP + 1) * P], Wo[:, i, :],
                                    start=(i == 0), stop=(i == 2 * REP - 1))
                return last
            pe.step([(scaled, (t, 1)), (w_in["wo"], (1, 1))] + free, mm, wo_done, t)
            r = t % PAY_RING
            pay = PAY[:, r, :]
            xr = pay[:, ROW_X:ROW_X + P]
            used = [(pay_out[r], t - PAY_RING), (x1_out[r], t - PAY_RING)] if t >= PAY_RING else [(empty_in, "all")]
            dve.step([(wo_done, t), (prep_v, ("gate", 3))] + used, lambda e: e.tensor_tensor(
                xr, ps[:, 0:P], mod[:, b, 0, :], ALU.mult), tail_v, ("ga", t))
            banks.read_by(n, (tail_v, ("ga", t)))
            dve.step([(tail_v, ("ga", t))], lambda e: e.tensor_tensor(xr, xr, x_sb[:, t, :], ALU.add), tail_v, ("x1", t))
            sp.step([(tail_v, ("x1", t))], lambda e: e.dma_start(out[t * P:(t + 1) * P, :], xr), x1_out[r], t)
            dve.step([(tail_v, ("x1", t))], lambda e: e.bn_stats(stats2[:, :], xr), tail_v, ("stats", t))
            dve.step([(tail_v, ("stats", t))], lambda e: e.bn_aggr(mv2[:, t, :], stats2[:, :]), tail_v, ("mv", t))
            pool.step([(tail_v, ("mv", t))], lambda e: e.tensor_scalar(
                var2[:, t:t + 1], mv2[:, t, 1:2], EPS, 1.0, ALU.add, ALU.mult), ln2_p, ("var", t))
            pool.step([(ln2_p, ("var", t))], lambda e: e.tensor_tensor(
                rstd2[:, t:t + 1], var2[:, t:t + 1], neg_half[:, 0:1], ALU.pow), ln2_p, ("rstd", t))

        def normalise2(t):
            b = t // BATCH_TILES
            pay = PAY[:, t % PAY_RING, :]
            xr, hr = pay[:, ROW_X:ROW_X + P], pay[:, ROW_H:ROW_H + P]
            dve.step([(ln2_p, ("rstd", t))], lambda e: e.tensor_scalar(
                hr, xr, mv2[:, t, 0:1], rstd2[:, t:t + 1], ALU.subtract, ALU.mult), tail_v, ("n", t))
            dve.step([(tail_v, ("n", t))], lambda e: e.tensor_tensor(hr, hr, mod[:, b, 2, :], ALU.mult), tail_v, ("m", t))
            dve.step([(tail_v, ("m", t))], lambda e: e.tensor_tensor(hr, hr, mod[:, b, 1, :], ALU.add), tail_v, ("h2", t))

        def turn_h2(t):
            n, ps, free = banks.take()
            pe.step([(tail_v, ("h2", t))] + free, lambda e: e.transpose(
                ps[:, 0:P], PAY[:, t % PAY_RING, ROW_H:ROW_H + P], ident[:, :]), h2_turned, t)
            act.step([(h2_turned, t)] + ([(logits_done, t - 1)] if t else []),
                     lambda e: e.activation(h2T[:, :], ps[:, 0:P], ACT.Copy), h2_kept, t)
            banks.read_by(n, (h2_kept, t))

        def route(t):
            n, ps, free = banks.take()
            pe.step([(h2_kept, t), (w_in["rest"], 3)] + free, lambda e: e.matmul(
                ps[:, 0:EXPERTS], h2T[:, :], Wg[:, :], start=True, stop=True), logits_done, t)
            lg = logits[:, t, :]
            dve.step([(logits_done, t)], lambda e: e.tensor_copy(lg, ps[:, 0:EXPERTS]), route_v, ("l", t))
            banks.read_by(n, (route_v, ("l", t)))
            dve.step([(route_v, ("l", t))], lambda e: e.max(top[:, t, :], lg), route_v, ("top", t))
            dve.step([(route_v, ("top", t))], lambda e: e.max_index(top_at[:, t, :], top[:, t, :], lg), route_v, ("at", t))
            dve.step([], lambda e: e.tensor_scalar(neg_top[:, t:t + 1], top[:, t, 0:1], -1.0, None, ALU.mult),
                     route_v, ("neg", t))
            dve.step([(route_v, ("at", t))], lambda e: e.tensor_scalar(
                onehot[:, t, :], iota8[:, :], top_at[:, t, 0:1], None, ALU.is_equal), route_v, ("one", t))
            dve.step([(route_v, ("one", t))], lambda e: e.tensor_tensor(
                seen[:, t + 1, :], seen[:, t, :], onehot[:, t, :], ALU.add), route_v, ("seen", t))
            act.step([(route_v, ("neg", t))] + ([(gate_e, t - 1)] if t else []), lambda e: e.activation(
                e8[:, :], lg, ACT.Exp, bias=neg_top[:, t:t + 1], accum_out=e_sum[:, t:t + 1]), gate_e, t)

        def gate_row(t):
            dve.step([(gate_e, t)], lambda e: e.reciprocal(gate[:, t:t + 1], e_sum[:, t:t + 1]), route_v, ("gate", t))
            b = t // BATCH_TILES
            dve.step([(route_v, ("gate", t))], lambda e: e.tensor_scalar(
                PAY[:, t % PAY_RING, ROW_G:ROW_G + P], mod[:, b, 3, :], gate[:, t:t + 1], None, ALU.mult),
                route_v, ("g", t))

        def place(t):
            n, ps, free = banks.take()

            def mm(e):
                e.matmul(ps[:, 0:EXPERTS], earlier_b[:, :], onehot[:, t, :], start=True, stop=False)
                return e.matmul(ps[:, 0:EXPERTS], ones_b[:, :], seen[:, t, :], start=False, stop=True)
            pe.step([(route_v, ("one", t))] + free, mm, placed, t)
            one = slice(t, t + 1)
            dve.step([(placed, t)], lambda e: e.tensor_tensor_reduce(
                out=prod8[:, :], in0=ps[:, 0:EXPERTS], in1=onehot[:, t, :], scale=1.0, scalar=0.0,
                op0=ALU.mult, op1=ALU.add, accum_out=loc[:, one]), route_v, ("loc", t))
            banks.read_by(n, (route_v, ("loc", t)))
            dve.step([(route_v, ("loc", t))], lambda e: e.scalar_tensor_tensor(
                slot[:, one], top_at[:, t, 0:1], float(CAP), loc[:, one], ALU.mult, ALU.add), route_v, ("slot", t))
            dve.step([], lambda e: e.tensor_scalar(
                over[:, one], loc[:, one], float(CAP), float(2 * TOKENS), ALU.is_ge, ALU.mult), route_v, ("over", t))
            dve.step([(route_v, ("over", t))], lambda e: e.tensor_tensor(
                slot_i[:, one], slot[:, one], over[:, one], ALU.add), route_v, ("slot_i", t))
            r = t % PAY_RING
            used = [(pay_out[r], t - PAY_RING)] if t >= PAY_RING else []
            pool.step(used, lambda e: e.tensor_copy(PAY[:, r, ROW_ID:ROW_ID + 1].bitcast(I32), tok_id[:, one]),
                      payload_p, t)
            pool.step([(payload_p, t), (route_v, ("slot_i", t)), (empty_in, "all")], lambda e: e.indirect_dma_start(
                sorted_rows, bass.IndirectOffsetOnAxis(ap=slot_i[:, one], axis=0), PAY[:, r, :], None,
                bounds_check=TOKENS - 1, oob_is_err=False), pay_out[r], t)

        ln1(0)
        normalise1(0)
        turn_x(0)
        split(WvH[:, :], WvL[:, :], stage_v, "wv", [(w_in["wv"], "in")])
        project_k(0, 0)
        split(WqH[:, :], WqL[:, :], stage_q, "wq", [(w_in["wq"], "in")])
        project_k(0, 1)
        project_v(0)
        for g in range(KV):
            project_q(0, g)
        finish_modulation()
        sp.step([(split_l, "wq"), (split_l, "wv"), (split_l, "wk"), (prep_t, BATCHES - 1)],
                lambda e: e.dma_start(w1_sb, w1.rearrange("e h f -> h e f")), w_in["w1"], "in")

        ln1(1)
        normalise1(1)
        for t in range(TILES + 3):
            k = t // 2 + 1
            more = k < BLOCKS and t < TILES
            even = t % 2 == 0
            now, last, third = t < TILES, 0 <= t - 1 < TILES, 0 <= t - 3 < TILES
            second = 0 <= t - 2 < TILES
            if now:
                scores(t, 0)
            if last:
                attend(t - 1, 1)
            if third:
                normalise2(t - 3)
            if last:
                sums(t - 1)
            if more:
                if even:
                    turn_x(k)
                else:
                    project_q(k, 0)
            if second:
                scale(t - 2, 0)
                scale(t - 2, 1)
            if more and not even:
                project_q(k, 1)
            if now:
                scores(t, 1)
            if third:
                turn_h2(t - 3)
            if last:
                invert(t - 1)
            if more:
                if even:
                    project_k(k, 0)
                    project_k(k, 1)
                else:
                    project_q(k, 2)
                    if k + 1 < BLOCKS:
                        ln1(k + 1)
            if third:
                route(t - 3)
            if second:
                out_project(t - 2)
            if now:
                attend(t, 0)
            if more:
                if even:
                    project_v(k)
                else:
                    project_q(k, 3)
                    if k + 1 < BLOCKS:
                        normalise1(k + 1)
            if third:
                gate_row(t - 3)
                place(t - 3)

        turn_banks = [turns[:, n, :] for n in (0, 1)]
        up_banks = [own[:, 0, :], own[:, 1, :], turns[:, 2, :], turns[:, 3, :]]
        down_banks = [turns[:, n, :] for n in (4, 5)]
        sorted_v = sorted_rows.rearrange("(e s p) r -> e p s r", s=ST, p=P)

        def load_rows(e_):
            waits = [(pay_out[t % PAY_RING], t) for t in range(TILES - PAY_RING, TILES)] + [(empty_in, "all")]
            waits += [(tail_v, ("x1", TILES - 1)), (scored, (TILES - 1, 1))]
            sp.step(waits, lambda e: e.dma_start(rows[e_], sorted_v[e_]), rows_in[e_], e_)

        def turn_rows(e_):
            ps = turn_banks[e_ % 2]

            def turn(e):
                for s in range(ST):
                    last = e.transpose(ps[:, s * P:(s + 1) * P], rows[e_][:, s, ROW_H:ROW_H + P], ident[:, :])
                return last
            free = [(xT_kept, e_ - 2)] if e_ >= 2 else banks.readers[e_]
            pe.step([(rows_in[e_], e_)] + free, turn, rows_turned, e_)
            act.step([(rows_turned, e_)] + ([(up_done, (e_ - 2, FC - 1))] if e_ >= 2 else [(scaled, (TILES - 1, 1))]),
                     lambda e: e.activation(xT[:, e_ % 2, :], ps, ACT.Copy), xT_kept, e_)

        def up(e_):
            for f in range(FC):
                free = [(relu_done, (e_ - 1, f))] if e_ else [(tanhed, (TILES - 1, 1))] + banks.readers[f]
                pe.step([(xT_kept, e_), (w_in["w1"], "in")] + free, lambda e, f=f: e.matmul(
                    up_banks[f], w1_sb[:, e_, f * P:(f + 1) * P], xT[:, e_ % 2, :], start=True, stop=True),
                    up_done, (e_, f))
                used = [(down_done, e_ - 2)] if e_ >= 2 else [(summed, TILES - 1), (pv_done, (TILES - 1, 1)),
                                                             (masked, (TILES - 1, 1))]
                act.step([(up_done, (e_, f)), (w_in["rest"], 3)] + used, lambda e, f=f: e.activation(
                    hidden[e_ % 2][:, f, :], up_banks[f], ACT.Relu, bias=b1_col[:, e_, f:f + 1]), relu_done, (e_, f))

        def down(e_):
            ps = down_banks[e_ % 2]

            def mm(e):
                for s in range(ST):
                    for f in range(FC):
                        last = e.matmul(ps[:, s * P:(s + 1) * P], hidden[e_ % 2][:, f, s * P:(s + 1) * P],
                                        W2[:, e_, f, :], start=(f == 0), stop=(f == FC - 1))
                return last
            free = [(out_v, (e_ - 2, "b2"))] if e_ >= 2 else banks.readers[4 + e_]
            pe.step([(relu_done, (e_, FC - 1))] + free, mm, down_done, e_)
            dst, rw = done_rows[e_ % 2], rows[e_]
            used = [(final_out[e_ % 2], (e_ - 2, ST - 1))] if e_ >= 2 else [(pv_done, (TILES - 1, 1))]
            dve.step([(down_done, e_), (w_in["b2"], "in")] + used, lambda e: e.tensor_tensor(
                dst, ps.rearrange("p (s d) -> p s d", s=ST), b2_row[:, e_, :].unsqueeze(1).to_broadcast([P, ST, P]),
                ALU.add), out_v, (e_, "b2"))
            dve.step([(out_v, (e_, "b2"))], lambda e: e.tensor_tensor(dst, dst, rw[:, :, ROW_G:ROW_G + P], ALU.mult),
                     out_v, (e_, "g"))
            dve.step([(out_v, (e_, "g"))], lambda e: e.tensor_tensor(dst, dst, rw[:, :, ROW_X:ROW_X + P], ALU.add),
                     out_v, (e_, "x"))
            for s in range(ST):
                waits = [(out_v, (e_, "x"))] + [(x1_out[t % PAY_RING], t) for t in range(TILES - PAY_RING, TILES)]
                pool.step(waits, lambda e, s=s: e.indirect_dma_start(
                    out, bass.IndirectOffsetOnAxis(ap=rw[:, s, ROW_ID:ROW_ID + 1].bitcast(I32), axis=0),
                    dst[:, s, :], None, bounds_check=TOKENS - 1, oob_is_err=False), final_out[e_ % 2], (e_, s))

        sp.step([(pv_done, (TILES - 1, 1))], lambda e: e.dma_start(
            b2_row, b2.unsqueeze(0).to_broadcast([P, EXPERTS, P])), w_in["b2"], "in")
        for e_ in range(EXPERTS):
            load_rows(e_)
        turn_rows(0)
        up(0)
        for e_ in range(1, EXPERTS):
            turn_rows(e_)
            up(e_)
            down(e_ - 1)
        down(EXPERTS - 1)
        sp.items.append(([(final_out[n].sem, final_out[n].count) for n in range(2)], lambda e: None, None))

        block = ctx.enter_context(nc.Block())
        block.sync(sp.run)
        block.tensor(pe.run)
        block.scalar(act.run)
        block.vector(dve.run)
        block.gpsimd(pool.run)


def kernel(L0_attn_x, L0_attn_Wq, L0_attn_Wk, L0_attn_Wv, L0_attn_Wo, L0_ffn_Wg, L0_ffn_W1, L0_ffn_b1,
           L0_ffn_W2, L0_ffn_b2, L0_c, L0_wmod):
    import concourse.bacc as bacc
    from concourse.bass_utils import run_bass_kernel_spmd

    ascon = np.ascontiguousarray
    arrays = {
        "x": ascon(L0_attn_x).reshape(TOKENS, P),
        "wq": ascon(np.transpose(L0_attn_Wq)),
        "wk": ascon(np.transpose(L0_attn_Wk)),
        "wv": ascon(np.transpose(L0_attn_Wv)),
        "wo": ascon(np.transpose(L0_attn_Wo)),
        "wg": ascon(L0_ffn_Wg),
        "w1": ascon(L0_ffn_W1),
        "b1": ascon(np.transpose(np.reshape(L0_ffn_b1, (EXPERTS, FC, P)), (2, 0, 1))),
        "w2": ascon(L0_ffn_W2),
        "b2": ascon(L0_ffn_b2),
        "c": ascon(np.transpose(L0_c)),
        "wmod": ascon(L0_wmod),
    }
    nc = bacc.Bacc("TRN2", target_bir_lowering=False, num_devices=1)
    args = [nc.dram_tensor(f"{n}_dram", a.shape, F32, kind="ExternalInput").ap() for n, a in arrays.items()]
    out = nc.dram_tensor("out_dram", (TOKENS, P), F32, kind="ExternalOutput").ap()
    build(nc, *args, out)
    r = run_bass_kernel_spmd(nc, [{f"{n}_dram": a for n, a in arrays.items()}], core_ids=[0])
    return r.results[0]["out_dram"].reshape(BATCHES, SEQ, P)
```

```python
from contextlib import ExitStack

import numpy as np

import concourse.bass as bass
from concourse import mybir

F32 = mybir.dt.float32
F32R = mybir.dt.float32r
BF16 = mybir.dt.bfloat16
I32 = mybir.dt.int32
U32 = mybir.dt.uint32
ALU = mybir.AluOpType
ACT = mybir.ActivationFunctionType

P = 128
BATCHES = 4
SEQ = 1024
HEADS, KV, D = 16, 4, 64
REP = HEADS // KV
SOFTCAP = 30.0
SCORE_SCALE = 1.0 / (D ** 0.5 * SOFTCAP)
EPS = 1e-5
EXPERTS, FF = 8, 512
FC = FF // P
TOKENS = BATCHES * SEQ
TILES = TOKENS // P
BATCH_TILES = SEQ // P
BLOCKS = TILES // 2
BT = 2 * P
CAP = TOKENS // EXPERTS
ST = CAP // P
HALF = P // 2

ROW_H, ROW_G, ROW_X, ROW_ID, ROW = 0, P, 2 * P, 3 * P, 400
NO_TOKEN = 1 << 20

TURNS = 6
K_RING, T_RING, V_RING, VD_RING, P_RING, PM_RING, PAY_RING = 3, 2, 6, 4, 4, 3, 3


SLOT = 14.0
PLAN = {
    "sp w1": 11.79, "sp x1": 41.11,
    "pe columns": -62.53, "pe mod": -39.2, "pe x turn": -31.05, "pe k0": -19.27, "pe q1": -17.74, "pe k1": -15.4,
    "pe q0": -11.18, "pe v": -10.91, "pe q2": -7.48, "pe q3": -3.69, "pe own 0": -0.6, "pe before 0": -0.09,
    "pe own 1": 5.97, "pe before 1": 6.1, "pe pv 0": 12.29, "pe sums": 13.77, "pe sums turn": 14.93,
    "pe pv 1": 16.85, "pe rs turn 0": 19.19, "pe rs turn 1": 19.59, "pe wo": 23.12, "pe h2 turn": 27.96,
    "pe logits": 29.12, "pe count": 41.79,
    "act wk": -83.32, "act mod": -57.58, "act wq1": -34.85, "act xh": -30.47, "act wq0": -26.56, "act wv": -24.64,
    "act k0": -15.71, "act q1 0": -15.43, "act q1 1": -14.78, "act k1": -14.36, "act q0 1": -10.74,
    "act q0 0": -9.83, "act v": -8.98, "act q2 1": -7.16, "act q2 0": -4.46, "act q3 0": -4.05, "act q3 1": -3.43,
    "act tanh 0": 3.35, "act exp 0": 4.56, "act tanh 1": 9.91, "act exp 1": 9.97, "act ou 0": 15.68,
    "act sums": 16.28, "act ou 1": 19.06, "act h2": 30.42, "act gate": 35.06,
    "dve stats1 1": -87.78, "dve columns": -75.95, "dve mv1 1": -65.79, "dve stats1 0": -64.82, "dve mv1 0": -63.9,
    "dve norm1 1": -42.85, "dve norm1 0": -38.04, "dve wk": -34.62, "dve wq1": -30.33, "dve xf": -29.53,
    "dve wq0": -24.84, "dve xl": -21.79, "dve mod": -20.12, "dve k0": -16.25, "dve wv": -16.08, "dve q1 1": -16.07,
    "dve q1 0": -14.97, "dve k1": -13.41, "dve q0 1": -8.98, "dve q0 0": -8.02, "dve q2 0": -3.84, "dve q2 1": -2.43,
    "dve q3 0": -2.09, "dve q3 1": -2.09, "dve merge 0 0": 1.07, "dve merge 0 1": 3.63, "dve merge 1 0": 6.91,
    "dve merge 1 1": 7.84, "dve invert": 16.54, "dve scale 0": 19.39, "dve scale 1": 20.54, "dve ga": 23.12,
    "dve x1": 24.0, "dve stats2": 24.39, "dve mv2": 25.49, "dve n": 28.0, "dve m": 28.17, "dve h2": 28.82,
    "dve l": 32.07, "dve top": 32.42, "dve at": 32.83, "dve neg": 32.84, "dve one": 34.73, "dve gate": 36.18,
    "dve seen": 38.86, "dve loc": 43.5, "dve g": 44.08, "dve over": 46.21, "dve slot": 46.45, "dve slot_i": 49.32,
    "pool var1": -67.12, "pool rstd1": -67.07, "pool vd 1": -11.58, "pool vd 0": -5.67, "pool mask 0": 1.87,
    "pool mask 1": 13.29, "pool repeat": 14.8, "pool id": 16.91, "pool var2": 16.99, "pool rstd2": 23.74,
    "pool scatter": 57.58,
}


class Signal:

    def __init__(self, sem, unit=1):
        self.sem, self.unit, self.count, self.at = sem, unit, 0, {}

    def next(self, key):
        self.count += self.unit
        self.at[key] = self.count


class Bank:

    def __init__(self, banks):
        self.banks, self.n, self.readers = banks, None, []

    @property
    def ps(self):
        return self.banks[:, self.n, :]

    def read_by(self, *who):
        self.readers += who


class Step:
    def __init__(self, when, waits, emit, signal, key, bank):
        self.when, self.waits, self.emit, self.done, self.key, self.bank = when, waits, emit, signal, key, bank


class Queue:

    def __init__(self):
        self.steps, self.part = [], 0

    def step(self, when, waits, emit, signal=None, key=None, bank=None):
        time = float("-inf") if when is None else when[0] * SLOT + PLAN[when[1]]
        s = Step((self.part, time), waits, emit, signal, key, bank)
        s.name = when
        self.steps.append(s)

    def order(self):
        self.steps.sort(key=lambda s: s.when)

    def count(self):
        for s in self.steps:
            if s.done is not None:
                s.done.next(s.key)

    def run(self, engine):
        passed = {}
        for s in self.steps:
            needed = {}
            for sig, key in s.waits:
                value = sig.at[key]
                if passed.get(id(sig), 0) < value:
                    passed[id(sig)] = value
                    needed[id(sig)] = (sig.sem, value)
            for sem, value in needed.values():
                engine.wait_ge(sem, value)
            last = s.emit(engine)
            if s.done is not None:
                last.then_inc(s.done.sem, s.done.unit)


def place_banks(pe):
    holder = [None] * TURNS
    turn = 0
    for s in pe.steps:
        if s.bank is not None:
            if holder[turn] is not None:
                s.waits = s.waits + holder[turn].readers
            s.bank.n, holder[turn] = turn, s.bank
            turn = (turn + 1) % TURNS
    return holder


def build(nc, x, wq, wk, wv, wo, wg, w1, b1, w2, b2, c, wmod, out):
    sorted_rows = nc.dram_tensor("sorted_rows", [TOKENS, ROW], F32, kind="Internal").ap()
    ctx = ExitStack()
    with ctx:
        def sb(name, shape, dt=F32):
            return ctx.enter_context(nc.sbuf_tensor(name, shape, dt))

        def pb(name, shape):
            return ctx.enter_context(nc.psum_tensor(name, shape, F32))

        def signal(name, unit=1):
            return Signal(ctx.enter_context(nc.semaphore(name)), unit)

        x_sb = sb("x_sb", [P, TILES, P])
        T = sb("T", [P, T_RING, HEADS, BT], F32R)
        KH = sb("KH", [P, K_RING, KV, BT], F32R)
        KL = sb("KL", [P, K_RING, KV, BT], F32R)
        V = sb("V", [P, V_RING, KV * D])
        VD = sb("VD", [P, VD_RING, KV * D])
        PR = sb("PR", [P, P_RING, 2 * REP * P])
        PM = sb("PM", [P, PM_RING, 2 * REP * P])
        OU = sb("OU", [P, 4, REP * P])
        ON = sb("ON", [P, 2, REP * P])
        SUMS = sb("SUMS", [P, REP * P])
        RS = sb("RS", [P, HEADS])
        RX = sb("RX", [P, HEADS, D])
        w_stage = sb("w_stage", [P, EXPERTS * FF])
        WqH, WqL = sb("WqH", [P, HEADS * D], F32R), sb("WqL", [P, HEADS * D], F32R)
        WkH, WkL = sb("WkH", [P, KV, 2, D], F32R), sb("WkL", [P, KV, 2, D], F32R)
        WvH, WvL = sb("WvH", [P, KV * D], F32R), sb("WvL", [P, KV * D], F32R)
        Wo = sb("Wo", [P, 2 * REP, P])
        Wg = sb("Wg", [P, EXPERTS])
        W2 = sb("W2", [P, EXPERTS, FC, P])
        b1_col = sb("b1_col", [P, EXPERTS, FC])
        cT = sb("cT", [P, BATCHES])
        c_e = sb("c_e", [P, BATCHES])
        c_r = sb("c_r", [P, BATCHES])
        siluT = sb("siluT", [P, BATCHES])
        sa_col = sb("sa_col", [P, BATCHES])
        ca_col = sb("ca_col", [P, BATCHES])
        mod = sb("mod", [P, BATCHES, 4, P])
        XN = sb("XN", [P, BT])
        XF = sb("XF", [P, BT])
        XH, XL = sb("XH", [P, 2, BT], F32R), sb("XL", [P, 2, BT], F32R)
        stats1, mv1 = sb("stats1", [P, 2, 6]), sb("mv1", [P, TILES, 2])
        stats2, mv2 = sb("stats2", [P, 6]), sb("mv2", [P, TILES, 2])
        var1, rstd1 = sb("var1", [P, TILES]), sb("rstd1", [P, TILES])
        var2, rstd2 = sb("var2", [P, TILES]), sb("rstd2", [P, TILES])
        PAY = sb("PAY", [P, PAY_RING, ROW])
        h2T = sb("h2T", [P, P])
        logits, e8 = sb("logits", [P, TILES, 8]), sb("e8", [P, 8])
        top, top_at = sb("top", [P, TILES, 8]), sb("top_at", [P, TILES, 8], U32)
        neg_top, e_sum, gate = sb("neg_top", [P, TILES]), sb("e_sum", [P, TILES]), sb("gate", [P, TILES])
        onehot = sb("onehot", [P, TILES, EXPERTS], BF16)
        seen = sb("seen", [P, TILES + 1, EXPERTS], BF16)
        prod8 = sb("prod8", [P, EXPERTS])
        loc, slot, over = sb("loc", [P, TILES]), sb("slot", [P, TILES]), sb("over", [P, TILES])
        slot_i = sb("slot_i", [P, TILES], I32)
        zeros = sb("zeros", [P, P])
        ident = sb("ident", [P, P])
        before = sb("before", [P, P])
        earlier = ON[:, 1, 0:P]
        earlier_b = sb("earlier_b", [P, P], BF16)
        ones_b = sb("ones_b", [P, P], BF16)
        ones32 = sb("ones32", [P, 32])
        neg_half = sb("neg_half", [P, 2])
        iota8i, iota8 = sb("iota8i", [P, EXPERTS], I32), sb("iota8", [P, EXPERTS])
        tok_id = sb("tok_id", [P, TILES], I32)
        empty_row = PAY[:, PAY_RING - 1, :]
        rows = []
        for wide in (x_sb[:, :, :].rearrange("p a b -> p (a b)"), T[:, :, :, :].rearrange("p a b c -> p (a b c)").bitcast(F32),
                     KH[:, :, :, :].rearrange("p a b c -> p (a b c)").bitcast(F32)):
            for i in range(wide.shape[1] // (ST * ROW)):
                rows.append(wide[:, i * ST * ROW:(i + 1) * ST * ROW].rearrange("p (s r) -> p s r", r=ROW))
        w1_sb = w_stage[:, :].rearrange("p (e f) -> p e f", e=EXPERTS)
        hidden = [PR[:, 2 * n:2 * n + 2, :].rearrange("p a (b s) -> p (a b) s", s=CAP) for n in range(2)]
        xT = OU
        b2_row = V[:, 0:4, :].rearrange("p a (b n) -> p (a b) n", n=P)
        done_rows = [PM[:, n, 0:ST * P].rearrange("p (s d) -> p s d", s=ST) for n in range(2)]

        own = pb("own", [P, 2, REP * P])
        turns = pb("turns", [P, TURNS, 512])

        x_in = [signal(f"x_in{b}", 16) for b in range(BATCHES)]
        w_in = {n: signal(f"{n}_in", 16) for n in ("wk", "wq", "wv", "c", "wmod", "wo", "w1", "b2", "rest")}
        empty_in = signal("empty_in", 16)
        pay_out = [signal(f"pay_out{n}", 16) for n in range(PAY_RING)]
        x1_out = [signal(f"x1_out{n}", 16) for n in range(PAY_RING)]
        rows_in = [signal(f"rows_in{n}", 16) for n in range(EXPERTS)]
        final_out = [signal(f"final_out{n}", 16) for n in range(2)]
        consts, consts_v = signal("consts"), signal("consts_v")
        prep_a, prep_v, prep_t = signal("prep_a"), signal("prep_v"), signal("prep_t")
        split_h, split_l = signal("split_h"), signal("split_l")
        ln1_v, ln1_p, normed1 = signal("ln1_v"), signal("ln1_p"), signal("normed1")
        x_turned, xh_done, xf_done, xl_done = (signal(n) for n in ("x_turned", "xh_done", "xf_done", "xl_done"))
        projected, h_kept, l_kept = signal("projected"), signal("h_kept"), signal("l_kept")
        v_kept, vd_done = signal("v_kept"), signal("vd_done")
        scored, merged, tanhed, exped, masked = (signal(n) for n in ("scored", "merged", "tanhed", "exped", "masked"))
        pv_done, o_kept, summed, sums_kept = (signal(n) for n in ("pv_done", "o_kept", "summed", "sums_kept"))
        sums_turned, inverted, repeated, rs_turned = (signal(n) for n in ("sums_turned", "inverted", "repeated", "rs_turned"))
        scaled, wo_done, tail_v, ln2_p, payload_p = (signal(n) for n in ("scaled", "wo_done", "tail_v", "ln2_p", "payload_p"))
        h2_turned, h2_kept, logits_done, gate_e, placed = (signal(n) for n in ("h2_turned", "h2_kept", "logits_done", "gate_e", "placed"))
        route_v = signal("route_v")
        rows_turned, xT_kept, up_done, relu_done, down_done, out_v = (
            signal(n) for n in ("rows_turned", "xT_kept", "up_done", "relu_done", "down_done", "out_v"))

        sp, pe, act, dve, pool = engines = [Queue() for _ in range(5)]

        x_v = x.rearrange("(b t p) d -> b p t d", t=BATCH_TILES, p=P)

        def load(dst, src, s, key="in"):
            sp.step(None, [], lambda e: e.dma_start(dst, src), s, key)

        stage_q = w_stage[:, 0:HEADS * D]
        stage_k = w_stage[:, 1024:1024 + 2 * KV * D].rearrange("p (g a d) -> p g a d", g=KV, a=2)
        stage_v = w_stage[:, 2048:2048 + KV * D]
        stage_m = w_stage[:, 3072:3072 + 6 * P]
        load(x_sb[:, 0:BATCH_TILES, :], x_v[0], x_in[0])
        load(cT[:, :], c, w_in["c"])
        load(stage_m, wmod, w_in["wmod"])
        for a in range(2):
            load(stage_k[:, :, a, :], wk.rearrange("p (g d) -> p g d", g=KV), w_in["wk"], a)
        load(stage_v, wv, w_in["wv"])
        load(stage_q, wq, w_in["wq"])
        for b in range(1, BATCHES):
            load(x_sb[:, b * BATCH_TILES:(b + 1) * BATCH_TILES, :], x_v[b], x_in[b])
        wo_v = wo.rearrange("(p h r d) n -> h d p r n", p=2, h=2, r=REP)
        for h in range(2):
            for p in range(2):
                load(Wo[h * HALF:(h + 1) * HALF, p * REP:(p + 1) * REP, :], wo_v[h, :, p], w_in["wo"], (h, p))
        load(Wg[:, :], wg, w_in["rest"], 0)
        load(b1_col[:, :, :], b1, w_in["rest"], 1)
        load(W2[:, :, :, :].rearrange("p e c n -> p (e c) n"), w2.rearrange("e (c p) n -> p (e c) n", p=P),
             w_in["rest"], 3)

        def const(emit, key, waits=()):
            pool.step(None, [(consts, k) for k in waits], emit, consts, key)

        const(lambda e: e.memset(zeros[:, :], 0.0), "zeros")
        const(lambda e: e.memset(ones32[:, :], 1.0), "ones32")
        const(lambda e: e.memset(ones_b[:, :], 1.0), "ones_b")
        const(lambda e: e.memset(neg_half[:, :], -0.5), "neg_half")
        const(lambda e: e.memset(seen[:, 0, :], 0.0), "seen")
        const(lambda e: e.memset(PAY[:, :, :], 0.0), "empty0")
        const(lambda e: e.affine_select(out=ident[:, :], in_=zeros[:, :], compare_op=ALU.not_equal, fill=1.0,
                                        base=0, pattern=[[-1, P]], channel_multiplier=1), "ident", ["zeros"])
        const(lambda e: e.affine_select(out=before[:, :], in_=zeros[:, :], compare_op=ALU.is_ge, fill=1.0,
                                        base=0, pattern=[[1, P]], channel_multiplier=-1), "before")
        const(lambda e: e.affine_select(out=earlier, in_=zeros[:, :], compare_op=ALU.is_ge, fill=1.0,
                                        base=0, pattern=[[-1, P]], channel_multiplier=1), "earlier")
        const(lambda e: e.memset(empty_row[:, ROW_ID:ROW_ID + 1].bitcast(I32), NO_TOKEN), "empty", ["empty0"])
        const(lambda e: e.iota(iota8i[:, :], pattern=[[1, EXPERTS]], base=0, channel_multiplier=0), "iota8i")
        const(lambda e: e.iota(tok_id[:, :], pattern=[[P, TILES]], base=0, channel_multiplier=1), "tok_id")
        const(lambda e: e.tensor_copy(iota8[:, :], iota8i[:, :]), "iota8", ["iota8i"])
        const(lambda e: e.tensor_copy(earlier_b[:, :], earlier), "earlier_b", ["earlier"])
        all_consts = (consts, "earlier_b")

        sp.step(None, [all_consts],
                lambda e: e.dma_start(sorted_rows.rearrange("(n p) r -> p n r", p=P),
                                      empty_row.unsqueeze(1).to_broadcast([P, TILES, ROW])), empty_in, "all")

        act.step(None, [(w_in["c"], "in")], lambda e: e.activation(c_e[:, :], cT[:, :], ACT.Exp, scale=-1.0), prep_a, "exp")
        dve.step(None, [(prep_a, "exp")], lambda e: e.tensor_scalar(c_e[:, :], c_e[:, :], 1.0, None, ALU.add), prep_v, "1+e")
        dve.step(None, [(prep_v, "1+e")], lambda e: e.reciprocal(c_r[:, :], c_e[:, :]), prep_v, "r")
        dve.step(None, [(prep_v, "r")], lambda e: e.tensor_tensor(siluT[:, :], cT[:, :], c_r[:, :], ALU.mult),
                 prep_v, "silu")

        columns = Bank(turns)

        def mod_columns(e):
            for j in range(2):
                last = e.matmul(columns.ps[:, 4 * j:4 * j + BATCHES], stage_m[:, j * P:(j + 1) * P], siluT[:, :],
                                start=True, stop=True)
            return last
        pe.step((0, "pe columns"), [(prep_v, "silu"), (w_in["wmod"], "in")], mod_columns, prep_t, "columns", columns)
        dve.step((0, "dve columns"), [(prep_t, "columns")],
                 lambda e: e.tensor_copy(sa_col[:, :], columns.ps[:, 0:BATCHES]), prep_v, "sa")
        dve.step((0, "dve columns"), [(prep_t, "columns")],
                 lambda e: e.tensor_scalar(ca_col[:, :], columns.ps[:, 4:4 + BATCHES], 1.0, None, ALU.add), prep_v, "ca")
        columns.read_by((prep_v, "ca"))
        for b in range(BATCHES):
            rows_of_mod = Bank(turns)
            pe.step((0, "pe mod"), [(prep_v, "silu"), (w_in["wmod"], "in")],
                    lambda e, b=b, bank=rows_of_mod: e.matmul(
                        bank.ps, siluT[:, b:b + 1].to_broadcast([P, P]), stage_m[:, 2 * P:6 * P], start=True, stop=True),
                    prep_t, b, rows_of_mod)
            act.step((0, "act mod"), [(prep_t, b)], lambda e, b=b, bank=rows_of_mod: e.activation(
                mod[:, b, :, :].rearrange("p j n -> p (j n)"), bank.ps, ACT.Copy), prep_a, b)
            rows_of_mod.read_by((prep_a, b))
        dve.step((0, "dve mod"), [(prep_a, BATCHES - 1)],
                 lambda e: e.tensor_scalar(mod[:, :, 2, :], mod[:, :, 2, :], 1.0, None, ALU.add), prep_v, "cb")
        for j in (0, 3):
            sign = PM[:, 0, 0:BATCHES * P].rearrange("p (b n) -> p b n", b=BATCHES)
            size = PM[:, 1, 0:BATCHES * P].rearrange("p (b n) -> p b n", b=BATCHES)
            g = mod[:, :, j, :]
            dve.step((0, "dve mod"), [(prep_a, BATCHES - 1)] + ([(prep_v, ("gate", 0))] if j else []),
                     lambda e, g=g, sign=sign: e.tensor_scalar(sign, g, 0.0, 0.5, ALU.is_ge, ALU.subtract),
                     prep_v, ("sign", j))
            dve.step((0, "dve mod"), [], lambda e, g=g, size=size: e.scalar_tensor_tensor(
                size, g, -1.0, g, ALU.mult, ALU.max), prep_v, ("size", j))
            dve.step((0, "dve mod"), [(prep_v, ("size", j))], lambda e, sign=sign, size=size: e.scalar_tensor_tensor(
                size, size, 0.25, sign, ALU.max, ALU.mult), prep_v, ("half", j))
            dve.step((0, "dve mod"), [(prep_v, ("half", j))], lambda e, g=g, size=size: e.tensor_scalar(
                g, size, 2.0, None, ALU.mult), prep_v, ("gate", j))

        def split(H, L, src, name, waits):
            act.step((0, "act " + name), waits, lambda e: e.activation(H, src, ACT.Copy), split_h, name)
            dve.step((0, "dve " + name), [(split_h, name)],
                     lambda e: e.tensor_tensor(L, src, H.bitcast(F32), ALU.subtract), split_l, name)

        split(WkH[:, :, :, :].rearrange("p g a d -> p (g a d)"), WkL[:, :, :, :].rearrange("p g a d -> p (g a d)"),
              w_stage[:, 1024:1024 + 2 * KV * D], "wk", [(w_in["wk"], 1)])
        split(WvH[:, :], WvL[:, :], stage_v, "wv", [(w_in["wv"], "in")])
        for i in range(2):
            half = slice(i * HEADS * D // 2, (i + 1) * HEADS * D // 2)
            split(WqH[:, half], WqL[:, half], stage_q[:, half], f"wq{i}", [(w_in["wq"], "in")])
        sp.step((0, "sp w1"), [(split_l, n) for n in ("wk", "wv", "wq0", "wq1")] + [(prep_t, n) for n in ("columns", *range(BATCHES))],
                lambda e: e.dma_start(w1_sb, w1.rearrange("e h f -> h e f")), w_in["w1"], "in")

        def ln1(k):
            tiles = (2 * k, 2 * k + 1)
            for j, t in enumerate(tiles):
                dve.step((2 * k, f"dve stats1 {j}"),
                         [(x_in[t // BATCH_TILES], "in")] + ([(ln1_v, ("mv", t - 2))] if t >= 2 else []),
                         lambda e, t=t: e.bn_stats(stats1[:, t % 2, :], x_sb[:, t, :]), ln1_v, ("stats", t))
            for j, t in enumerate(tiles):
                dve.step((2 * k, f"dve mv1 {j}"), [(ln1_v, ("stats", t))],
                         lambda e, t=t: e.bn_aggr(mv1[:, t, :], stats1[:, t % 2, :]), ln1_v, ("mv", t))
            s = slice(2 * k, 2 * k + 2)
            pool.step((2 * k, "pool var1"), [(ln1_v, ("mv", t)) for t in tiles], lambda e: e.tensor_scalar(
                var1[:, s], mv1[:, s, 1], EPS, 1.0, ALU.add, ALU.mult), ln1_p, ("var", k))
            pool.step((2 * k, "pool rstd1"), [(ln1_p, ("var", k))], lambda e: e.tensor_tensor(
                rstd1[:, s], var1[:, s], neg_half[:, :], ALU.pow), ln1_p, ("rstd", k))
            for j, t in enumerate(tiles):
                dve.step((2 * k, f"dve norm1 {j}"), [(ln1_p, ("rstd", k))] + ([(x_turned, k - 1)] if k else []),
                         lambda e, t=t, j=j: e.tensor_scalar(
                             XN[:, j * P:(j + 1) * P], x_sb[:, t, :], mv1[:, t, 0:1], rstd1[:, t:t + 1],
                             ALU.subtract, ALU.mult), normed1, t)

        def turn_x(k):
            b = 2 * k // BATCH_TILES
            bank = Bank(turns)

            def turn(e):
                for j in range(2):
                    last = e.transpose(bank.ps[:, j * P:(j + 1) * P], XN[:, j * P:(j + 1) * P], ident[:, :])
                return last
            pe.step((2 * k, "pe x turn"), [(normed1, 2 * k), (normed1, 2 * k + 1), all_consts], turn, x_turned, k, bank)
            used = [(projected, (k - 2, n)) for n in ("v", "k0", "k1", "q0", "q1", "q2", "q3")] if k >= 2 else []
            act.step((2 * k, "act xh"), [(x_turned, k), (prep_v, "sa"), (prep_v, "ca")] + used, lambda e: e.activation(
                XH[:, k % 2, :], bank.ps[:, 0:BT], ACT.Identity, bias=sa_col[:, b:b + 1], scale=ca_col[:, b:b + 1]),
                xh_done, k)
            dve.step((2 * k, "dve xf"), [(xh_done, k)] + ([(xl_done, k - 1)] if k else []), lambda e: e.tensor_scalar(
                XF[:, :], bank.ps[:, 0:BT], ca_col[:, b:b + 1], sa_col[:, b:b + 1], ALU.mult, ALU.add), xf_done, k)
            dve.step((2 * k, "dve xl"), [(xf_done, k)], lambda e: e.tensor_tensor(
                XL[:, k % 2, :], XF[:, :], XH[:, k % 2, :].bitcast(F32), ALU.subtract), xl_done, k)
            bank.read_by((xh_done, k), (xf_done, k))

        def three_passes(e, dst, wh, wl, xh, xl):
            e.matmul(dst, wh, xh, start=True, stop=False)
            e.matmul(dst, wh, xl, start=False, stop=False)
            return e.matmul(dst, wl, xh, start=False, stop=True)

        def project_k(k, i):
            bank, name = Bank(turns), f"k{i}"

            def pair():
                return bank.ps.rearrange("p (g n) -> p g n", g=2)

            def mm(e):
                for a in range(2):
                    last = three_passes(e, pair()[:, a, :], WkH[:, 2 * i + a, :, :].rearrange("p a d -> p (a d)"),
                                        WkL[:, 2 * i + a, :, :].rearrange("p a d -> p (a d)"),
                                        XH[:, k % 2, :], XL[:, k % 2, :])
                return last
            pe.step((2 * k, "pe " + name), [(xl_done, k), (split_l, "wk")], mm, projected, (k, name), bank)
            used = [(scored, (2 * k - 4, h)) for h in range(2)] if k >= 3 else []
            kh, kl = KH[:, k % K_RING, 2 * i:2 * i + 2, :], KL[:, k % K_RING, 2 * i:2 * i + 2, :]
            act.step((2 * k, "act " + name), [(projected, (k, name))] + used,
                     lambda e: e.activation(kh, pair(), ACT.Copy), h_kept, (k, name))
            dve.step((2 * k, "dve " + name), [(h_kept, (k, name))],
                     lambda e: e.tensor_tensor(kl, pair(), kh.bitcast(F32), ALU.subtract), l_kept, (k, name))
            bank.read_by((l_kept, (k, name)))

        def project_v(k):
            bank = Bank(turns)

            def mm(e):
                for j in range(2):
                    tok = slice(j * P, (j + 1) * P)
                    dst = bank.ps[:, j * BT:(j + 1) * BT]
                    e.matmul(dst, XH[:, k % 2, tok], WvH[:, :], start=True, stop=False)
                    e.matmul(dst, XL[:, k % 2, tok], WvH[:, :], start=False, stop=False)
                    last = e.matmul(dst, XH[:, k % 2, tok], WvL[:, :], start=False, stop=True)
                return last
            pe.step((2 * k, "pe v"), [(xl_done, k), (split_l, "wv")], mm, projected, (k, "v"), bank)
            used = [(pv_done, (2 * k - 4, h)) for h in range(2)] if k >= 3 else []
            r = 2 * k % V_RING
            act.step((2 * k, "act v"), [(projected, (k, "v"))] + used, lambda e: e.activation(
                V[:, r:r + 2, :], bank.ps.rearrange("p (t n) -> p t n", t=2), ACT.Copy), v_kept, k)
            bank.read_by((v_kept, k))
            for j, t in enumerate((2 * k, 2 * k + 1)):
                if t % BATCH_TILES:
                    used = [(pv_done, (t - VD_RING, h)) for h in range(2)] if t >= VD_RING else []
                    pool.step((2 * k, f"pool vd {j}"), [(v_kept, k)] + used, lambda e, t=t: e.tensor_tensor(
                        VD[:, t % VD_RING, :], V[:, t % V_RING, :], V[:, (t - 1) % V_RING, :], ALU.subtract),
                        vd_done, t)

        def project_q(k, g):
            bank, name = Bank(turns), f"q{g}"

            def mm(e):
                for a in range(2):
                    w = slice((2 * g + a) * P, (2 * g + a + 1) * P)
                    last = three_passes(e, bank.ps[:, a * BT:(a + 1) * BT], WqH[:, w], WqL[:, w],
                                        XH[:, k % 2, :], XL[:, k % 2, :])
                return last
            pe.step((2 * k, "pe " + name), [(xl_done, k), (split_l, f"wq{g // 2}")], mm, projected, (k, name), bank)
            used = [(scored, (2 * k - 3, h)) for h in range(2)] if k >= 2 else []
            halves = (slice(0, HALF), slice(HALF, P))

            def head_pairs(half):
                return bank.ps[half, :].rearrange("p (c n) -> p c n", c=2)
            for odd in range(2):
                mine, other = halves[odd], halves[1 - odd]
                act.step((2 * k, f"act {name} {odd}"), [(projected, (k, name))] + used,
                         lambda e, odd=odd, mine=mine: e.activation(
                             T[mine, k % T_RING, 4 * g + odd:4 * g + 4:2, :], head_pairs(mine), ACT.Copy),
                         h_kept, (k, name, odd))
                dve.step((2 * k, f"dve {name} {odd}"), [(h_kept, (k, name, odd))],
                         lambda e, odd=odd, mine=mine, other=other: e.tensor_tensor(
                             T[other, k % T_RING, 4 * g + odd:4 * g + 4:2, :], head_pairs(mine),
                             T[mine, k % T_RING, 4 * g + odd:4 * g + 4:2, :].bitcast(F32), ALU.subtract),
                         l_kept, (k, name, odd))
                bank.read_by((l_kept, (k, name, odd)))

        def scores(t, h):
            k, first, u = t // 2, t % BATCH_TILES == 0, 2 * t + h
            last_unit = (t, 0) if h else (t - 1, 1)

            def pair(e, dst, key_tile, g):
                q = T[:, k % T_RING, 4 * g:4 * g + 4, (t % 2) * P:(t % 2 + 1) * P]
                at = slice(key_tile % 2 * P, (key_tile % 2 + 1) * P)
                e.matmul(dst, KH[:, key_tile // 2 % K_RING, g, at], q, start=True, stop=False)
                return e.matmul(dst, KL[:, key_tile // 2 % K_RING, g, at], q, start=False, stop=True)

            for a in range(2):
                g = 2 * h + a
                pe.step((t, f"pe own {h}"), [(l_kept, (k, f"k{h}")), (l_kept, (k, f"q{g}", 0)), (l_kept, (k, f"q{g}", 1))]
                        + ([(tanhed, last_unit)] if u else []),
                        lambda e, a=a, g=g: pair(e, own[:, a, :], t, g), scored, (t, h) if first and a else (t, h, "own", a))
            if not first:
                for a in range(2):
                    g = 2 * h + a
                    bank = Bank(turns)
                    pe.step((t, f"pe before {h}"), [(l_kept, (k, f"q{g}", 0)), (l_kept, (k, f"q{g}", 1))],
                            lambda e, g=g, bank=bank: pair(e, bank.ps, t - 1, g),
                            scored, (t, h) if a else (t, h, "before"), bank)
                    dve.step((t, f"dve merge {h} {a}"), [(scored, (t, h, "own", a)), (scored, (t, h) if a else (t, h, "before"))],
                             lambda e, a=a, bank=bank: e.copy_predicated(
                                 own[:, a, :].rearrange("p (r n) -> p r n", n=P),
                                 before[:, :].bitcast(U32).unsqueeze(1).to_broadcast([P, REP, P]),
                                 bank.ps.rearrange("p (r n) -> p r n", n=P)), merged, (t, h, a))
                    bank.read_by((merged, (t, h, a)))
            source = [(scored, (t, h))] if first else [(merged, (t, h, 0)), (merged, (t, h, 1))]
            pr, pm = PR[:, u % P_RING, :], PM[:, u % PM_RING, :]
            used = [(summed, t - 2), (pv_done, (t - 2, h)), (masked, (t - 2, h))] if t >= 2 else []
            act.step((t, f"act tanh {h}"), source + used, lambda e: e.activation(
                pr, own[:, :, :].rearrange("p a n -> p (a n)"), ACT.Tanh, scale=SCORE_SCALE), tanhed, (t, h))
            act.step((t, f"act exp {h}"), [(tanhed, (t, h))],
                     lambda e: e.activation(pr, pr, ACT.Exp, scale=SOFTCAP), exped, (t, h))
            used = [(prep_v, ("gate", 3))]
            if u >= PM_RING:
                ot, oh = divmod(u - PM_RING, 2)
                used.append((pv_done, (ot, oh)))
                if ot % BATCH_TILES == 0:
                    used.append((summed, ot))
            pool.step((t, f"pool mask {h}"), [(exped, (t, h))] + used, lambda e: e.affine_select(
                out=pm.rearrange("p (r n) -> p r n", n=P), in_=pr.rearrange("p (r n) -> p r n", n=P),
                compare_op=ALU.is_ge, fill=0.0, base=0, pattern=[[0, 2 * REP], [1, P]], channel_multiplier=-1),
                masked, (t, h))

        def attend(t, h):
            first, u = t % BATCH_TILES == 0, 2 * t + h
            bank = Bank(turns)

            def mm(e):
                parts = [(V, PM, u % PM_RING, t % V_RING)] if first else [
                    (V, PR, u % P_RING, (t - 1) % V_RING), (VD, PM, u % PM_RING, t % VD_RING)]
                for m, (v, p, pr, vr) in enumerate(parts):
                    for a in range(2):
                        g = 2 * h + a
                        last = e.matmul(bank.ps[a * HALF:(a + 1) * HALF, :], v[:, vr, g * D:(g + 1) * D],
                                        p[:, pr, a * REP * P:(a + 1) * REP * P],
                                        start=(m == 0), stop=(m == len(parts) - 1))
                return last
            ready = [(masked, (t, h)), (v_kept, t // 2)] + ([] if first else [(vd_done, t)])
            pe.step((t, f"pe pv {h}"), ready, mm, pv_done, (t, h), bank)
            act.step((t, f"act ou {h}"), [(pv_done, (t, h))] + ([(scaled, (t - 2, h))] if t >= 2 else []),
                     lambda e: e.activation(OU[:, u % 4, :], bank.ps, ACT.Copy), o_kept, (t, h))
            bank.read_by((o_kept, (t, h)))

        def sums(t):
            first = t % BATCH_TILES == 0
            bank = Bank(turns)

            def mm(e):
                for g in range(KV):
                    u = 2 * t + g // 2
                    p = PM[:, u % PM_RING, :] if first else PR[:, u % P_RING, :]
                    last = e.matmul(bank.ps[32 * g:32 * g + 32, :], ones32[:, :],
                                    p[:, (g % 2) * REP * P:(g % 2 + 1) * REP * P], start=True, stop=True,
                                    tile_position=(0, 32 * g))
                return last
            pe.step((t, "pe sums"), [(masked if first else exped, (t, h)) for h in range(2)], mm, summed, t, bank)
            act.step((t, "act sums"), [(summed, t)] + ([(sums_turned, t - 1)] if t else []),
                     lambda e: e.activation(SUMS[:, :], bank.ps, ACT.Copy), sums_kept, t)
            bank.read_by((sums_kept, t))

        def invert(t):
            bank = Bank(turns)

            def turn(e):
                for r in range(REP):
                    last = e.transpose(bank.ps[:, r * P:(r + 1) * P], SUMS[:, r * P:(r + 1) * P], ident[:, :])
                return last
            pe.step((t, "pe sums turn"), [(sums_kept, t)], turn, sums_turned, t, bank)
            dve.step((t, "dve invert"), [(sums_turned, t)] + ([(repeated, t - 1)] if t else []), lambda e: e.reciprocal(
                RS[:, :].rearrange("q (p r h) -> q r p h", p=2, r=REP),
                bank.ps[:, 0:REP * P:32].rearrange("q (r p h) -> q r p h", r=REP, p=2)), inverted, t)
            bank.read_by((inverted, t))
            pool.step((t, "pool repeat"), [(inverted, t)] + ([(rs_turned, (t - 1, h)) for h in range(2)] if t else []),
                      lambda e: e.tensor_scalar(
                          RX[:, :, :], RS[:, :].unsqueeze(2).to_broadcast([P, HEADS, D]), 1.0, 1.0, ALU.mult, ALU.mult),
                      repeated, t)

        def scale(t, h):
            bank = Bank(turns)

            def turn(e):
                for r in range(REP):
                    i = 2 * (h * REP + r)
                    last = e.transpose(bank.ps[:, r * P:(r + 1) * P], RX[:, i:i + 2, :].rearrange("q a d -> q (a d)"),
                                       ident[:, :])
                return last
            pe.step((t, f"pe rs turn {h}"), [(repeated, t)], turn, rs_turned, (t, h), bank)
            dve.step((t, f"dve scale {h}"), [(rs_turned, (t, h)), (o_kept, (t, h))] + ([(wo_done, t - 1)] if t else []),
                     lambda e: e.tensor_tensor(ON[:, h, :], bank.ps, OU[:, (2 * t + h) % 4, :], ALU.mult), scaled, (t, h))
            bank.read_by((scaled, (t, h)))

        def out_project(t):
            b = t // BATCH_TILES
            bank = Bank(turns)

            def mm(e):
                for i in range(2 * REP):
                    last = e.matmul(bank.ps[:, 0:P], ON[:, i // REP, (i % REP) * P:(i % REP + 1) * P], Wo[:, i, :],
                                    start=(i == 0), stop=(i == 2 * REP - 1))
                return last
            pe.step((t, "pe wo"), [(scaled, (t, 0)), (scaled, (t, 1)), (w_in["wo"], (1, 1))], mm, wo_done, t, bank)
            r = t % PAY_RING
            xr = PAY[:, r, ROW_X:ROW_X + P]
            used = [(pay_out[r], t - PAY_RING), (x1_out[r], t - PAY_RING)] if t >= PAY_RING else [(empty_in, "all")]
            dve.step((t, "dve ga"), [(wo_done, t), (prep_v, ("gate", 3))] + used, lambda e: e.tensor_tensor(
                xr, bank.ps[:, 0:P], mod[:, b, 0, :], ALU.mult), tail_v, ("ga", t))
            bank.read_by((tail_v, ("ga", t)))
            dve.step((t, "dve x1"), [(tail_v, ("ga", t))], lambda e: e.tensor_tensor(xr, xr, x_sb[:, t, :], ALU.add),
                     tail_v, ("x1", t))
            sp.step((t, "sp x1"), [(tail_v, ("x1", t))],
                    lambda e: e.dma_start(out[t * P:(t + 1) * P, :], xr), x1_out[r], t)
            dve.step((t, "dve stats2"), [(tail_v, ("x1", t))] + ([(tail_v, ("mv", t - 1))] if t else []),
                     lambda e: e.bn_stats(stats2[:, :], xr), tail_v, ("stats", t))
            dve.step((t, "dve mv2"), [(tail_v, ("stats", t))],
                     lambda e: e.bn_aggr(mv2[:, t, :], stats2[:, :]), tail_v, ("mv", t))
            pool.step((t, "pool var2"), [(tail_v, ("mv", t))], lambda e: e.tensor_scalar(
                var2[:, t:t + 1], mv2[:, t, 1:2], EPS, 1.0, ALU.add, ALU.mult), ln2_p, ("var", t))
            pool.step((t, "pool rstd2"), [(ln2_p, ("var", t))], lambda e: e.tensor_tensor(
                rstd2[:, t:t + 1], var2[:, t:t + 1], neg_half[:, 0:1], ALU.pow), ln2_p, ("rstd", t))

        def normalise2(t):
            b = t // BATCH_TILES
            pay = PAY[:, t % PAY_RING, :]
            xr, hr = pay[:, ROW_X:ROW_X + P], pay[:, ROW_H:ROW_H + P]
            dve.step((t, "dve n"), [(ln2_p, ("rstd", t))], lambda e: e.tensor_scalar(
                hr, xr, mv2[:, t, 0:1], rstd2[:, t:t + 1], ALU.subtract, ALU.mult), tail_v, ("n", t))
            dve.step((t, "dve m"), [(tail_v, ("n", t))],
                     lambda e: e.tensor_tensor(hr, hr, mod[:, b, 2, :], ALU.mult), tail_v, ("m", t))
            dve.step((t, "dve h2"), [(tail_v, ("m", t))],
                     lambda e: e.tensor_tensor(hr, hr, mod[:, b, 1, :], ALU.add), tail_v, ("h2", t))
            bank = Bank(turns)
            pe.step((t, "pe h2 turn"), [(tail_v, ("h2", t))], lambda e: e.transpose(bank.ps[:, 0:P], hr, ident[:, :]),
                    h2_turned, t, bank)
            act.step((t, "act h2"), [(h2_turned, t)] + ([(logits_done, t - 1)] if t else []),
                     lambda e: e.activation(h2T[:, :], bank.ps[:, 0:P], ACT.Copy), h2_kept, t)
            bank.read_by((h2_kept, t))

        def route(t):
            b = t // BATCH_TILES
            bank = Bank(turns)
            pe.step((t, "pe logits"), [(h2_kept, t), (w_in["rest"], 3)], lambda e: e.matmul(
                bank.ps[:, 0:EXPERTS], h2T[:, :], Wg[:, :], start=True, stop=True), logits_done, t, bank)
            lg = logits[:, t, :]
            dve.step((t, "dve l"), [(logits_done, t)], lambda e: e.tensor_copy(lg, bank.ps[:, 0:EXPERTS]),
                     route_v, ("l", t))
            bank.read_by((route_v, ("l", t)))
            dve.step((t, "dve top"), [(route_v, ("l", t))], lambda e: e.max(top[:, t, :], lg), route_v, ("top", t))
            dve.step((t, "dve at"), [(route_v, ("top", t))], lambda e: e.max_index(top_at[:, t, :], top[:, t, :], lg),
                     route_v, ("at", t))
            dve.step((t, "dve neg"), [(route_v, ("top", t))], lambda e: e.tensor_scalar(
                neg_top[:, t:t + 1], top[:, t, 0:1], -1.0, None, ALU.mult), route_v, ("neg", t))
            dve.step((t, "dve one"), [(route_v, ("at", t))], lambda e: e.tensor_scalar(
                onehot[:, t, :], iota8[:, :], top_at[:, t, 0:1], None, ALU.is_equal), route_v, ("one", t))
            dve.step((t, "dve seen"), [(route_v, ("one", t))] + ([(route_v, ("seen", t - 1))] if t else []),
                     lambda e: e.tensor_tensor(seen[:, t + 1, :], seen[:, t, :], onehot[:, t, :], ALU.add),
                     route_v, ("seen", t))
            act.step((t, "act gate"), [(route_v, ("neg", t))] + ([(gate_e, t - 1)] if t else []), lambda e: e.activation(
                e8[:, :], lg, ACT.Exp, bias=neg_top[:, t:t + 1], accum_out=e_sum[:, t:t + 1]), gate_e, t)
            dve.step((t, "dve gate"), [(gate_e, t)], lambda e: e.reciprocal(gate[:, t:t + 1], e_sum[:, t:t + 1]),
                     route_v, ("gate", t))
            dve.step((t, "dve g"), [(route_v, ("gate", t))], lambda e: e.tensor_scalar(
                PAY[:, t % PAY_RING, ROW_G:ROW_G + P], mod[:, b, 3, :], gate[:, t:t + 1], None, ALU.mult),
                route_v, ("g", t))

        def place(t):
            bank = Bank(turns)

            def mm(e):
                e.matmul(bank.ps[:, 0:EXPERTS], earlier_b[:, :], onehot[:, t, :], start=True, stop=False)
                return e.matmul(bank.ps[:, 0:EXPERTS], ones_b[:, :], seen[:, t, :], start=False, stop=True)
            pe.step((t, "pe count"), [(route_v, ("one", t))] + ([(route_v, ("seen", t - 1))] if t else []),
                    mm, placed, t, bank)
            one = slice(t, t + 1)
            dve.step((t, "dve loc"), [(placed, t)] + ([(route_v, ("loc", t - 1))] if t else []),
                     lambda e: e.tensor_tensor_reduce(
                out=prod8[:, :], in0=bank.ps[:, 0:EXPERTS], in1=onehot[:, t, :], scale=1.0, scalar=0.0,
                op0=ALU.mult, op1=ALU.add, accum_out=loc[:, one]), route_v, ("loc", t))
            bank.read_by((route_v, ("loc", t)))
            dve.step((t, "dve slot"), [(route_v, ("loc", t))], lambda e: e.scalar_tensor_tensor(
                slot[:, one], top_at[:, t, 0:1], float(CAP), loc[:, one], ALU.mult, ALU.add), route_v, ("slot", t))
            dve.step((t, "dve over"), [(route_v, ("loc", t))], lambda e: e.tensor_scalar(
                over[:, one], loc[:, one], float(CAP), float(2 * TOKENS), ALU.is_ge, ALU.mult), route_v, ("over", t))
            dve.step((t, "dve slot_i"), [(route_v, ("over", t)), (route_v, ("slot", t))], lambda e: e.tensor_tensor(
                slot_i[:, one], slot[:, one], over[:, one], ALU.add), route_v, ("slot_i", t))
            r = t % PAY_RING
            used = [(pay_out[r], t - PAY_RING)] if t >= PAY_RING else [(empty_in, "all")]
            pool.step((t, "pool id"), used, lambda e: e.tensor_copy(
                PAY[:, r, ROW_ID:ROW_ID + 1].bitcast(I32), tok_id[:, one]), payload_p, t)
            waits = [(payload_p, t), (route_v, ("slot_i", t)), (route_v, ("g", t)), (empty_in, "all")]
            pool.step((t, "pool scatter"), waits, lambda e: e.indirect_dma_start(
                sorted_rows, bass.IndirectOffsetOnAxis(ap=slot_i[:, one], axis=0), PAY[:, r, :], None,
                bounds_check=TOKENS - 1, oob_is_err=False), pay_out[r], t)

        for k in range(BLOCKS):
            ln1(k)
            turn_x(k)
            for i in range(2):
                project_k(k, i)
            project_v(k)
            for g in range(KV):
                project_q(k, g)
        for t in range(TILES):
            for h in range(2):
                scores(t, h)
                attend(t, h)
            sums(t)
            invert(t)
            for h in range(2):
                scale(t, h)
            out_project(t)
            normalise2(t)
            route(t)
            place(t)
        for queue in engines:
            queue.order()
            queue.part += 1
        held = place_banks(pe)

        turn_banks = [turns[:, n, :] for n in (0, 1)]
        up_banks = [own[:, 0, :], own[:, 1, :], turns[:, 2, :], turns[:, 3, :]]
        down_banks = [turns[:, n, :] for n in (4, 5)]
        sorted_v = sorted_rows.rearrange("(e s p) r -> e p s r", s=ST, p=P)

        def load_rows(e_):
            waits = [(pay_out[t % PAY_RING], t) for t in range(TILES - PAY_RING, TILES)] + [(empty_in, "all")]
            waits += [(tail_v, ("x1", TILES - 1)), (scored, (TILES - 1, 1))]
            sp.step(None, waits, lambda e: e.dma_start(rows[e_], sorted_v[e_]), rows_in[e_], e_)

        def turn_rows(e_):
            ps = turn_banks[e_ % 2]

            def turn(e):
                for s in range(ST):
                    last = e.transpose(ps[:, s * P:(s + 1) * P], rows[e_][:, s, ROW_H:ROW_H + P], ident[:, :])
                return last
            free = [(xT_kept, e_ - 2)] if e_ >= 2 else held[e_].readers
            pe.step(None, [(rows_in[e_], e_)] + free, turn, rows_turned, e_)
            act.step(None, [(rows_turned, e_)] + ([(up_done, (e_ - 2, FC - 1))] if e_ >= 2 else [(scaled, (TILES - 1, 1))]),
                     lambda e: e.activation(xT[:, e_ % 2, :], ps, ACT.Copy), xT_kept, e_)

        def up(e_):
            for f in range(FC):
                free = [(relu_done, (e_ - 1, f))] if e_ else [(tanhed, (TILES - 1, 1))] + held[f].readers
                pe.step(None, [(xT_kept, e_), (w_in["w1"], "in")] + free, lambda e, f=f: e.matmul(
                    up_banks[f], w1_sb[:, e_, f * P:(f + 1) * P], xT[:, e_ % 2, :], start=True, stop=True),
                    up_done, (e_, f))
                used = [(down_done, e_ - 2)] if e_ >= 2 else [(summed, TILES - 1), (pv_done, (TILES - 1, 1)),
                                                             (masked, (TILES - 1, 1))]
                act.step(None, [(up_done, (e_, f)), (w_in["rest"], 3)] + used, lambda e, f=f: e.activation(
                    hidden[e_ % 2][:, f, :], up_banks[f], ACT.Relu, bias=b1_col[:, e_, f:f + 1]), relu_done, (e_, f))

        def down(e_):
            ps = down_banks[e_ % 2]

            def mm(e):
                for s in range(ST):
                    for f in range(FC):
                        last = e.matmul(ps[:, s * P:(s + 1) * P], hidden[e_ % 2][:, f, s * P:(s + 1) * P],
                                        W2[:, e_, f, :], start=(f == 0), stop=(f == FC - 1))
                return last
            free = [(out_v, (e_ - 2, "b2"))] if e_ >= 2 else held[4 + e_].readers
            pe.step(None, [(relu_done, (e_, FC - 1))] + free, mm, down_done, e_)
            dst, rw = done_rows[e_ % 2], rows[e_]
            used = [(final_out[e_ % 2], (e_ - 2, ST - 1))] if e_ >= 2 else [(pv_done, (TILES - 1, 1))]
            dve.step(None, [(down_done, e_), (w_in["b2"], "in")] + used, lambda e: e.tensor_tensor(
                dst, ps.rearrange("p (s d) -> p s d", s=ST), b2_row[:, e_, :].unsqueeze(1).to_broadcast([P, ST, P]),
                ALU.add), out_v, (e_, "b2"))
            dve.step(None, [(out_v, (e_, "b2"))], lambda e: e.tensor_tensor(dst, dst, rw[:, :, ROW_G:ROW_G + P], ALU.mult),
                     out_v, (e_, "g"))
            dve.step(None, [(out_v, (e_, "g"))], lambda e: e.tensor_tensor(dst, dst, rw[:, :, ROW_X:ROW_X + P], ALU.add),
                     out_v, (e_, "x"))
            for s in range(ST):
                waits = [(out_v, (e_, "x"))] + [(x1_out[t % PAY_RING], t) for t in range(TILES - PAY_RING, TILES)]
                pool.step(None, waits, lambda e, s=s: e.indirect_dma_start(
                    out, bass.IndirectOffsetOnAxis(ap=rw[:, s, ROW_ID:ROW_ID + 1].bitcast(I32), axis=0),
                    dst[:, s, :], None, bounds_check=TOKENS - 1, oob_is_err=False), final_out[e_ % 2], (e_, s))

        sp.step(None, [(pv_done, (TILES - 1, 1))], lambda e: e.dma_start(
            b2_row, b2.unsqueeze(0).to_broadcast([P, EXPERTS, P])), w_in["b2"], "in")
        for e_ in range(EXPERTS):
            load_rows(e_)
        turn_rows(0)
        up(0)
        for e_ in range(1, EXPERTS):
            turn_rows(e_)
            up(e_)
            down(e_ - 1)
        down(EXPERTS - 1)
        sp.step(None, [(final_out[n], (EXPERTS - 2 + n, ST - 1)) for n in range(2)], lambda e: None)
        for queue in engines:
            queue.count()

        block = ctx.enter_context(nc.Block())
        block.sync(sp.run)
        block.tensor(pe.run)
        block.scalar(act.run)
        block.vector(dve.run)
        block.gpsimd(pool.run)


def kernel(L0_attn_x, L0_attn_Wq, L0_attn_Wk, L0_attn_Wv, L0_attn_Wo, L0_ffn_Wg, L0_ffn_W1, L0_ffn_b1,
           L0_ffn_W2, L0_ffn_b2, L0_c, L0_wmod):
    import concourse.bacc as bacc
    from concourse.bass_utils import run_bass_kernel_spmd

    ascon = np.ascontiguousarray
    arrays = {
        "x": ascon(L0_attn_x).reshape(TOKENS, P),
        "wq": ascon(np.transpose(L0_attn_Wq)),
        "wk": ascon(np.transpose(L0_attn_Wk)),
        "wv": ascon(np.transpose(L0_attn_Wv)),
        "wo": ascon(np.transpose(L0_attn_Wo)),
        "wg": ascon(L0_ffn_Wg),
        "w1": ascon(L0_ffn_W1),
        "b1": ascon(np.transpose(np.reshape(L0_ffn_b1, (EXPERTS, FC, P)), (2, 0, 1))),
        "w2": ascon(L0_ffn_W2),
        "b2": ascon(L0_ffn_b2),
        "c": ascon(np.transpose(L0_c)),
        "wmod": ascon(L0_wmod),
    }
    nc = bacc.Bacc("TRN2", target_bir_lowering=False, num_devices=1)
    args = [nc.dram_tensor(f"{n}_dram", a.shape, F32, kind="ExternalInput").ap() for n, a in arrays.items()]
    out = nc.dram_tensor("out_dram", (TOKENS, P), F32, kind="ExternalOutput").ap()
    build(nc, *args, out)
    r = run_bass_kernel_spmd(nc, [{f"{n}_dram": a for n, a in arrays.items()}], core_ids=[0])
    return r.results[0]["out_dram"].reshape(BATCHES, SEQ, P)
```

```python
from contextlib import ExitStack

import numpy as np

import concourse.bass as bass
from concourse import mybir

F32 = mybir.dt.float32
F32R = mybir.dt.float32r
BF16 = mybir.dt.bfloat16
I32 = mybir.dt.int32
U32 = mybir.dt.uint32
ALU = mybir.AluOpType
ACT = mybir.ActivationFunctionType

P = 128
BATCHES = 4
SEQ = 1024
HEADS, KV, D = 16, 4, 64
REP = HEADS // KV
SOFTCAP = 30.0
SCORE_SCALE = 1.0 / (D ** 0.5 * SOFTCAP)
EPS = 1e-5
EXPERTS, FF = 8, 512
FC = FF // P
TOKENS = BATCHES * SEQ
TILES = TOKENS // P
BATCH_TILES = SEQ // P
BLOCKS = TILES // 2
BT = 2 * P
CAP = TOKENS // EXPERTS
ST = CAP // P
HALF = P // 2

ROW_H, ROW_G, ROW_X, ROW_ID, ROW = 0, P, 2 * P, 3 * P, 400
NO_TOKEN = 1 << 20

TURNS = 6
K_RING, T_RING, V_RING, VD_RING, P_RING, PM_RING, PAY_RING = 3, 2, 6, 4, 4, 3, 4


SLOT = 14.0
PLAN = {
    "sp mod": -32.56, "sp w1": -17.96, "sp x1": 66.03,
    "pe mod": -127.94, "pe columns": -109.07, "pe x turn": -34.72, "pe k": -23.56, "pe q1": -21.93, "pe q0": -11.62,
    "pe v": -11.31, "pe q3": -8.86, "pe q2": -7.55, "pe own 0": -5.1, "pe before 0": -0.14, "pe before 1": 3.35,
    "pe own 1": 5.93, "pe pv 0": 6.69, "pe sums": 13.78, "pe sums turn": 15.69, "pe pv 1": 16.94,
    "pe rs turn 0": 17.23, "pe rs turn 1": 17.97, "pe wo": 39.26, "pe y turn": 42.4, "pe h2 turn": 50.5,
    "pe logits": 57.1, "pe count": 61.95,
    "act wk": -177.96, "act wv": -120.74, "act wq1": -87.57, "act wq0": -57.59, "act mod": -56.79, "act xh": -30.85,
    "act k twice 1": -24.02, "act k 1": -16.56, "act k 0": -15.78, "act k twice 0": -15.32, "act q1 1": -15.21,
    "act q1 0": -14.41, "act q0 0": -11.69, "act q0 1": -11.3, "act v": -10.31, "act q3 1": -10.01, "act wo1": -9.96,
    "act q3 0": -4.71, "act q2 0": -4.35, "act q2 1": -3.0, "act tanh 0": 3.68, "act exp 0": 3.78,
    "act tanh 1": 10.24, "act exp 1": 10.89, "act ou 0": 13.98, "act sums": 14.06, "act wo0": 17.28,
    "act ou 1": 17.79, "act oh 0": 17.81, "act oh 1": 21.42, "act y": 41.79, "act h2": 54.77, "act gate": 71.18,
    "dve wq1": -111.53, "dve wk": -108.26, "dve stats1 0": -81.99, "dve stats1 1": -78.87, "dve mv1 0": -76.05,
    "dve mv1 1": -73.83, "dve norm1 1": -55.18, "dve columns": -51.18, "dve norm1 0": -48.25, "dve wv": -40.27,
    "dve wq0": -33.43, "dve mod": -29.53, "dve xf": -29.32, "dve xl": -28.5, "dve k 1": -16.44, "dve k 0": -16.13,
    "dve q1 1": -15.72, "dve q1 0": -14.58, "dve q0 0": -10.19, "dve q0 1": -9.89, "dve k twice 0": -8.17,
    "dve k twice 1": -6.14, "dve q3 0": -5.89, "dve q3 1": -2.93, "dve q2 0": -2.62, "dve q2 1": -1.7,
    "dve merge 0 0": -0.53, "dve merge 0 1": 0.45, "dve merge 1 0": 7.75, "dve merge 1 1": 7.84, "dve wo1": 8.3,
    "dve invert": 14.06, "dve scale 0": 19.95, "dve scale 1": 21.43, "dve wo0": 30.33, "dve ga": 44.11,
    "dve x1": 45.29, "dve stats2": 45.7, "dve mv2": 46.18, "dve n": 49.28, "dve m": 50.42, "dve h2": 51.46,
    "dve l": 58.72, "dve top": 59.48, "dve at": 60.54, "dve one": 63.28, "dve loc": 64.61, "dve slot": 66.3,
    "dve over": 67.98, "dve neg": 68.7, "dve gate": 71.13, "dve seen": 73.73, "dve g": 75.94, "dve slot_i": 80.77,
    "pool var1": -58.96, "pool rstd1": -58.86, "pool vd 0": -5.58, "pool vd 1": -3.23, "pool mask 0": 8.23,
    "pool mask 1": 10.79, "pool repeat": 11.95, "pool ol 0": 23.1, "pool ol 1": 23.82, "pool var2": 44.54,
    "pool rstd2": 44.83, "pool id": 56.69, "pool scatter": 80.63,
}
FIRST = {
    "sp x1": 70.5,
    "pe x turn": -72.5, "pe k": -50.95, "pe before 0": -47.4, "pe q1": -38.86, "pe q0": -36.94,
    "pe before 1": -32.95, "pe v": -28.3, "pe q2": -18.17, "pe q3": -9.13, "pe own 0": -2.4, "pe own 1": 3.22,
    "pe pv 0": 5.85, "pe sums": 13.06, "pe sums turn": 16.73, "pe pv 1": 17.37, "pe rs turn 0": 18.52,
    "pe rs turn 1": 29.51, "pe wo": 41.69, "pe y turn": 43.59, "pe h2 turn": 55.5, "pe logits": 58.18,
    "pe count": 66.75,
    "act xh": -78.06, "act k 0": -51.81, "act q1 0": -43.82, "act k twice 0": -32.63, "act k 1": -27.12,
    "act k twice 1": -24.04, "act q1 1": -23.76, "act q2 1": -19.7, "act q3 0": -19.54, "act q0 0": -15.49,
    "act q0 1": -12.35, "act v": -9.74, "act q2 0": -4.78, "act q3 1": -2.49, "act tanh 0": 2.22, "act exp 0": 2.23,
    "act tanh 1": 2.47, "act exp 1": 3.89, "act ou 0": 15.43, "act sums": 15.66, "act ou 1": 19.55,
    "act oh 0": 28.24, "act oh 1": 31.95, "act y": 41.96, "act h2": 56.48, "act gate": 71.28,
    "dve stats1 1": -206.71, "dve stats1 0": -157.13, "dve mv1 1": -136.88, "dve mv1 0": -120.47,
    "dve norm1 1": -90.86, "dve norm1 0": -70.64, "dve xf": -36.71, "dve xl": -36.63, "dve q1 0": -28.73,
    "dve k 0": -28.33, "dve k twice 0": -22.63, "dve k 1": -22.38, "dve k twice 1": -16.56, "dve q0 0": -15.37,
    "dve q0 1": -11.76, "dve q1 1": -11.32, "dve q3 0": -8.93, "dve q2 0": -5.24, "dve merge 0 0": -4.7,
    "dve q2 1": -4.65, "dve q3 1": -2.02, "dve merge 1 0": 0.9, "dve merge 1 1": 2.22, "dve invert": 17.54,
    "dve scale 0": 21.71, "dve scale 1": 31.23, "dve ga": 42.58, "dve x1": 42.72, "dve stats2": 42.92,
    "dve merge 0 1": 43.66, "dve mv2": 44.23, "dve n": 46.93, "dve m": 50.27, "dve h2": 51.37, "dve l": 57.67,
    "dve top": 57.93, "dve at": 58.48, "dve neg": 62.06, "dve one": 63.15, "dve seen": 64.48, "dve loc": 65.97,
    "dve slot": 68.68, "dve over": 69.85, "dve slot_i": 71.79, "dve gate": 71.92, "dve g": 74.65,
    "pool var1": -119.52, "pool rstd1": -107.55, "pool vd 1": -12.65, "pool mask 0": -11.79, "pool mask 1": 1.34,
    "pool repeat": 9.17, "pool ol 0": 31.91, "pool id": 36.41, "pool ol 1": 37.18, "pool var2": 42.82,
    "pool rstd2": 45.45, "pool vd 0": 46.47, "pool scatter": 75.28,
}
LAST = {
    "sp x1": 76.08,
    "pe x turn": -34.09, "pe k": -23.77, "pe q1": -21.86, "pe q0": -12.06, "pe v": -11.24, "pe q3": -9.38,
    "pe q2": -7.96, "pe own 0": -2.11, "pe before 0": -0.04, "pe before 1": 4.06, "pe own 1": 5.08, "pe pv 0": 6.25,
    "pe sums": 13.58, "pe sums turn": 16.75, "pe pv 1": 16.77, "pe rs turn 0": 16.86, "pe rs turn 1": 17.74,
    "pe wo": 38.42, "pe y turn": 40.58, "pe h2 turn": 50.19, "pe logits": 57.9, "pe count": 77.77,
    "act xh": -28.53, "act k 1": -20.71, "act k twice 1": -19.71, "act k twice 0": -19.13, "act q1 1": -17.6,
    "act q1 0": -17.41, "act k 0": -15.99, "act q0 0": -12.38, "act q0 1": -11.46, "act v": -11.45, "act q3 1": -6.7,
    "act q3 0": -4.08, "act q2 1": -3.29, "act q2 0": -1.43, "act tanh 0": 1.41, "act exp 0": 3.4,
    "act tanh 1": 10.25, "act exp 1": 10.6, "act ou 0": 13.78, "act sums": 13.88, "act ou 1": 17.5,
    "act oh 0": 18.04, "act oh 1": 21.4, "act y": 40.42, "act h2": 55.8, "act gate": 63.39,
    "dve stats1 1": -97.37, "dve stats1 0": -85.71, "dve mv1 1": -81.83, "dve mv1 0": -72.58, "dve norm1 0": -47.16,
    "dve norm1 1": -42.03, "dve xf": -29.1, "dve xl": -27.0, "dve k 1": -16.3, "dve q1 1": -15.71, "dve k 0": -15.34,
    "dve q1 0": -15.22, "dve k twice 0": -14.74, "dve q0 0": -10.67, "dve q0 1": -10.22, "dve k twice 1": -8.07,
    "dve q3 0": -3.67, "dve q3 1": -2.06, "dve q2 1": -1.63, "dve q2 0": -1.16, "dve merge 0 0": -0.4,
    "dve merge 0 1": -0.26, "dve merge 1 0": 7.96, "dve merge 1 1": 8.39, "dve invert": 14.42, "dve scale 0": 20.85,
    "dve scale 1": 20.93, "dve ga": 38.94, "dve x1": 39.27, "dve stats2": 39.41, "dve mv2": 40.5, "dve n": 48.59,
    "dve m": 48.88, "dve h2": 51.14, "dve l": 60.54, "dve top": 62.12, "dve neg": 63.56, "dve at": 66.71,
    "dve one": 69.14, "dve seen": 70.64, "dve gate": 71.37, "dve loc": 75.31, "dve g": 76.49, "dve over": 80.72,
    "dve slot": 81.42, "dve slot_i": 83.53,
    "pool var1": -68.6, "pool rstd1": -63.83, "pool vd 0": -8.87, "pool vd 1": -5.63, "pool mask 0": 4.27,
    "pool mask 1": 10.53, "pool repeat": 13.45, "pool ol 0": 21.61, "pool ol 1": 22.38, "pool id": 35.6,
    "pool var2": 39.67, "pool rstd2": 42.51, "pool scatter": 130.14,
}


class Signal:

    def __init__(self, sem, unit=1):
        self.sem, self.unit, self.count, self.at = sem, unit, 0, {}

    def next(self, key):
        self.count += self.unit
        self.at[key] = self.count


class Bank:

    def __init__(self, banks):
        self.banks, self.n, self.readers = banks, None, []

    @property
    def ps(self):
        return self.banks[:, self.n, :]

    def read_by(self, *who):
        self.readers += who


class Step:

    def __init__(self, when, waits, emit, signal, key, bank):
        self.when, self.waits, self.emit, self.done, self.key, self.bank = when, waits, emit, signal, key, bank


class Queue:

    def __init__(self):
        self.steps, self.part = [], 0

    def step(self, when, waits, emit, signal=None, key=None, bank=None):
        if when is None:
            time = float("-inf")
        else:
            tile, name = when
            own_plan = FIRST if tile == 0 else LAST if tile >= TILES - 4 else PLAN
            time = tile * SLOT + (own_plan[name] if name in own_plan else PLAN[name])
        self.steps.append(Step((self.part, time), waits, emit, signal, key, bank))

    def order(self):
        self.steps.sort(key=lambda s: s.when)

    def count(self):
        for s in self.steps:
            if s.done is not None:
                s.done.next(s.key)

    def run(self, engine):
        passed = {}
        for s in self.steps:
            needed = {}
            for sig, key in s.waits:
                value = sig.at[key]
                if passed.get(id(sig), 0) < value:
                    passed[id(sig)] = value
                    needed[id(sig)] = (sig.sem, value)
            for sem, value in needed.values():
                engine.wait_ge(sem, value)
            last = s.emit(engine)
            if s.done is not None:
                last.then_inc(s.done.sem, s.done.unit)


def place_banks(pe):
    holder = [None] * TURNS
    turn = 0
    for s in pe.steps:
        if s.bank is not None:
            if holder[turn] is not None:
                s.waits = s.waits + holder[turn].readers
            s.bank.n, holder[turn] = turn, s.bank
            turn = (turn + 1) % TURNS
    return holder


def build(nc, x, wq, wk, wv, wo, wg, w1, b1, w2, b2, c, wmod, out):
    sorted_rows = nc.dram_tensor("sorted_rows", [TOKENS, ROW], F32, kind="Internal").ap()
    mod_dram = nc.dram_tensor("mod_dram", [BATCHES, 4 * P], F32, kind="Internal").ap()
    ctx = ExitStack()
    with ctx:
        def sb(name, shape, dt=F32):
            return ctx.enter_context(nc.sbuf_tensor(name, shape, dt))

        def pb(name, shape):
            return ctx.enter_context(nc.psum_tensor(name, shape, F32))

        def signal(name, unit=1):
            return Signal(ctx.enter_context(nc.semaphore(name)), unit)

        x_sb = sb("x_sb", [P, TILES, P])
        T = sb("T", [P, T_RING, HEADS, BT], F32R)
        KH = sb("KH", [P, K_RING, KV, BT], F32R)
        KL = sb("KL", [P, K_RING, KV, BT], F32R)
        V = sb("V", [P, V_RING, KV * D])
        VD = sb("VD", [P, VD_RING, KV * D])
        PR = sb("PR", [P, P_RING, 2 * REP * P])
        PM = sb("PM", [P, PM_RING, 2 * REP * P])
        OU = sb("OU", [P, 4, REP * P])
        OH = sb("OH", [P, 2, 2, REP * P], F32R)
        OL = sb("OL", [P, 2, 2, REP * P], F32R)
        YT = sb("YT", [P, BT])
        SUMS = sb("SUMS", [P, REP * P])
        RS = sb("RS", [P, HEADS])
        RX = sb("RX", [P, HEADS, D])
        w_stage = sb("w_stage", [P, EXPERTS * FF])
        WqH, WqL = sb("WqH", [P, HEADS * D], F32R), sb("WqL", [P, HEADS * D], F32R)
        WkH, WkL = sb("WkH", [P, KV * D], F32R), sb("WkL", [P, KV * D], F32R)
        WvH, WvL = sb("WvH", [P, KV * D], F32R), sb("WvL", [P, KV * D], F32R)
        WoH, WoL = sb("WoH", [P, 2 * REP, P], F32R), sb("WoL", [P, 2 * REP, P], F32R)
        Wg = sb("Wg", [P, EXPERTS])
        b1_col = sb("b1_col", [P, EXPERTS, FC])
        cT = sb("cT", [P, BATCHES])
        c_e = sb("c_e", [P, BATCHES])
        c_r = sb("c_r", [P, BATCHES])
        siluT = sb("siluT", [P, BATCHES])
        sa_col = sb("sa_col", [P, BATCHES])
        ca_col = sb("ca_col", [P, BATCHES])
        mod = sb("mod", [P, BATCHES, 4, P])
        at_first = RX[0:BATCHES, :, :].rearrange("b (j h) d -> b j (h d)", h=P // D)
        mod4, sign4, size4 = at_first[:, 0:4, :], at_first[:, 4:6, :], at_first[:, 6:8, :]
        XN = sb("XN", [P, BT])
        XF = sb("XF", [P, BT])
        XH, XL = sb("XH", [P, 2, BT], F32R), sb("XL", [P, 2, BT], F32R)
        stats1, mv1 = sb("stats1", [P, 2, 6]), sb("mv1", [P, TILES, 2])
        stats2, mv2 = sb("stats2", [P, 6]), sb("mv2", [P, TILES, 2])
        var1, rstd1 = sb("var1", [P, TILES]), sb("rstd1", [P, TILES])
        var2, rstd2 = sb("var2", [P, TILES]), sb("rstd2", [P, TILES])
        PAY = sb("PAY", [P, PAY_RING, ROW])
        h2T = sb("h2T", [P, P])
        logits, e8 = sb("logits", [P, TILES, 8]), sb("e8", [P, 8])
        top, top_at = sb("top", [P, TILES, 8]), sb("top_at", [P, TILES, 8], U32)
        neg_top, e_sum, gate = sb("neg_top", [P, TILES]), sb("e_sum", [P, TILES]), sb("gate", [P, TILES])
        onehot = sb("onehot", [P, TILES, EXPERTS], BF16)
        seen = sb("seen", [P, TILES + 1, EXPERTS], BF16)
        prod8 = sb("prod8", [P, EXPERTS])
        loc, slot, over = sb("loc", [P, TILES]), sb("slot", [P, TILES]), sb("over", [P, TILES])
        slot_i = sb("slot_i", [P, TILES], I32)
        zeros = sb("zeros", [P, P])
        ident = sb("ident", [P, P])
        before = sb("before", [P, P])
        earlier = YT[:, 0:P]
        earlier_b = sb("earlier_b", [P, P], BF16)
        ones_b = sb("ones_b", [P, P], BF16)
        ones32 = sb("ones32", [P, 32])
        neg_half = sb("neg_half", [P, 2])
        iota8i, iota8 = sb("iota8i", [P, EXPERTS], I32), sb("iota8", [P, EXPERTS])
        tok_id = sb("tok_id", [P, TILES], I32)
        empty_row = PAY[:, PAY_RING - 1, :]
        rows = []
        for wide in (x_sb[:, :, :].rearrange("p a b -> p (a b)"), T[:, :, :, :].rearrange("p a b c -> p (a b c)").bitcast(F32),
                     KH[:, :, :, :].rearrange("p a b c -> p (a b c)").bitcast(F32)):
            for i in range(wide.shape[1] // (ST * ROW)):
                rows.append(wide[:, i * ST * ROW:(i + 1) * ST * ROW].rearrange("p (s r) -> p s r", r=ROW))
        W2 = [part.rearrange("p a (c n) -> p (a c) n", n=P) for part in (PM[:, 1:3, :], OU[:, :, :])]
        w1_sb = w_stage[:, :].rearrange("p (e f) -> p e f", e=EXPERTS)
        hidden = [PR[:, 2 * n:2 * n + 2, :].rearrange("p a (b s) -> p (a b) s", s=CAP) for n in range(2)]
        xTH, xTL = (KL[:, n, :, :].rearrange("p (a b) c -> p a (b c)", a=2) for n in range(2))
        w1H, w1L = (w[:, :].rearrange("p (n f) -> p n f", n=2) for w in (WqH, WqL))
        b2_row = V[:, 0:4, :].rearrange("p a (b n) -> p (a b) n", n=P)
        done_rows = [PM[:, 0, n * ST * P:(n + 1) * ST * P].rearrange("p (s d) -> p s d", s=ST) for n in range(2)]

        own = pb("own", [P, 2, REP * P])
        turns = pb("turns", [P, TURNS, 512])

        x_in = [signal(f"x_in{b}", 16) for b in range(BATCHES)]
        w_in = {n: signal(f"{n}_in", 16) for n in ("wk", "wq", "wv", "c", "wmod", "wo", "w1", "b2", "rest", "mod")}
        mod_out = signal("mod_out", 16)
        empty_in = signal("empty_in", 16)
        pay_out = [signal(f"pay_out{n}", 16) for n in range(PAY_RING)]
        x1_out = [signal(f"x1_out{n}", 16) for n in range(PAY_RING)]
        rows_in = [signal(f"rows_in{n}", 16) for n in range(EXPERTS)]
        w2_in = [signal(f"w2_in{n}", 16) for n in range(EXPERTS)]
        rest_in = signal("row_rest_in", 16)
        final_out = [signal(f"final_out{n}", 16) for n in range(2)]
        consts, consts_v = signal("consts"), signal("consts_v")
        prep_a, prep_v, prep_t = signal("prep_a"), signal("prep_v"), signal("prep_t")
        split_h, split_l = signal("split_h"), signal("split_l")
        ln1_v, ln1_p, normed1 = signal("ln1_v"), signal("ln1_p"), signal("normed1")
        x_turned, xh_done, xf_done, xl_done = (signal(n) for n in ("x_turned", "xh_done", "xf_done", "xl_done"))
        projected, h_kept, l_kept = signal("projected"), signal("h_kept"), signal("l_kept")
        v_kept, vd_done = signal("v_kept"), signal("vd_done")
        scored, merged, tanhed, exped, masked = (signal(n) for n in ("scored", "merged", "tanhed", "exped", "masked"))
        pv_done, o_kept, summed, sums_kept = (signal(n) for n in ("pv_done", "o_kept", "summed", "sums_kept"))
        sums_turned, inverted, repeated, rs_turned = (signal(n) for n in ("sums_turned", "inverted", "repeated", "rs_turned"))
        oh_done, ol_done, yT_kept, y_turned, scaled, wo_done, tail_v, ln2_p, payload_p = (signal(n) for n in ("oh_done", "ol_done", "yT_kept", "y_turned", "scaled", "wo_done", "tail_v", "ln2_p", "payload_p"))
        h2_turned, h2_kept, logits_done, gate_e, placed = (signal(n) for n in ("h2_turned", "h2_kept", "logits_done", "gate_e", "placed"))
        route_v = signal("route_v")
        rows_turned, xTH_kept, xTL_kept, w1H_kept, w1L_kept, up_done, relu_done, down_done, out_v = (
            signal(n) for n in ("rows_turned", "xTH_kept", "xTL_kept", "w1H_kept", "w1L_kept", "up_done", "relu_done",
                                "down_done", "out_v"))

        sp, pe, act, dve, pool = engines = [Queue() for _ in range(5)]

        x_v = x.rearrange("(b t p) d -> b p t d", t=BATCH_TILES, p=P)

        def load(dst, src, s, key="in"):
            sp.step(None, [], lambda e: e.dma_start(dst, src), s, key)

        stage_q = w_stage[:, 0:HEADS * D]
        stage_k = w_stage[:, HEADS * D:(HEADS + KV) * D]
        stage_v = w_stage[:, (HEADS + KV) * D:(HEADS + 2 * KV) * D]
        stage_m = w_stage[:, (HEADS + 2 * KV) * D:(HEADS + 2 * KV) * D + 6 * P]
        stage_o = w_stage[:, EXPERTS * FF - HEADS * D:EXPERTS * FF].rearrange("p (i n) -> p i n", n=P)
        load(x_sb[:, 0:BATCH_TILES, :], x_v[0], x_in[0])
        load(cT[:, :], c, w_in["c"])
        load(stage_m, wmod, w_in["wmod"])
        load(stage_k, wk, w_in["wk"])
        load(stage_v, wv, w_in["wv"])
        load(stage_q, wq, w_in["wq"])
        for b in range(1, BATCHES):
            load(x_sb[:, b * BATCH_TILES:(b + 1) * BATCH_TILES, :], x_v[b], x_in[b])
        wo_v = wo.rearrange("(p h r d) n -> h d p r n", p=2, h=2, r=REP)
        for h in range(2):
            for p in range(2):
                load(stage_o[h * HALF:(h + 1) * HALF, p * REP:(p + 1) * REP, :], wo_v[h, :, p], w_in["wo"], (h, p))
        load(Wg[:, :], wg, w_in["rest"], 0)
        load(b1_col[:, :, :], b1, w_in["rest"], 1)

        def const(emit, key, waits=()):
            pool.step(None, [(consts, k) for k in waits], emit, consts, key)

        const(lambda e: e.memset(zeros[:, :], 0.0), "zeros")
        const(lambda e: e.memset(ones32[:, :], 1.0), "ones32")
        const(lambda e: e.memset(ones_b[:, :], 1.0), "ones_b")
        const(lambda e: e.memset(neg_half[:, :], -0.5), "neg_half")
        const(lambda e: e.memset(seen[:, 0, :], 0.0), "seen")
        const(lambda e: e.memset(PAY[:, :, :], 0.0), "empty0")
        const(lambda e: e.affine_select(out=ident[:, :], in_=zeros[:, :], compare_op=ALU.not_equal, fill=1.0,
                                        base=0, pattern=[[-1, P]], channel_multiplier=1), "ident", ["zeros"])
        const(lambda e: e.affine_select(out=before[:, :], in_=zeros[:, :], compare_op=ALU.is_ge, fill=1.0,
                                        base=0, pattern=[[1, P]], channel_multiplier=-1), "before")
        const(lambda e: e.affine_select(out=earlier, in_=zeros[:, :], compare_op=ALU.is_ge, fill=1.0,
                                        base=0, pattern=[[-1, P]], channel_multiplier=1), "earlier")
        const(lambda e: e.memset(empty_row[:, ROW_ID:ROW_ID + 1].bitcast(I32), NO_TOKEN), "empty", ["empty0"])
        const(lambda e: e.iota(iota8i[:, :], pattern=[[1, EXPERTS]], base=0, channel_multiplier=0), "iota8i")
        const(lambda e: e.iota(tok_id[:, :], pattern=[[P, TILES]], base=0, channel_multiplier=1), "tok_id")
        const(lambda e: e.tensor_copy(iota8[:, :], iota8i[:, :]), "iota8", ["iota8i"])
        const(lambda e: e.tensor_copy(earlier_b[:, :], earlier), "earlier_b", ["earlier"])
        all_consts = (consts, "earlier_b")

        sp.step(None, [all_consts],
                lambda e: e.dma_start(sorted_rows.rearrange("(n p) r -> p n r", p=P),
                                      empty_row.unsqueeze(1).to_broadcast([P, TILES, ROW])), empty_in, "all")

        act.step(None, [(w_in["c"], "in")], lambda e: e.activation(c_e[:, :], cT[:, :], ACT.Exp, scale=-1.0), prep_a, "exp")
        dve.step(None, [(prep_a, "exp")], lambda e: e.tensor_scalar(c_e[:, :], c_e[:, :], 1.0, None, ALU.add), prep_v, "1+e")
        dve.step(None, [(prep_v, "1+e")], lambda e: e.reciprocal(c_r[:, :], c_e[:, :]), prep_v, "r")
        dve.step(None, [(prep_v, "r")], lambda e: e.tensor_tensor(siluT[:, :], cT[:, :], c_r[:, :], ALU.mult),
                 prep_v, "silu")

        columns = Bank(turns)

        def mod_columns(e):
            for j in range(2):
                last = e.matmul(columns.ps[:, 4 * j:4 * j + BATCHES], stage_m[:, j * P:(j + 1) * P], siluT[:, :],
                                start=True, stop=True)
            return last
        pe.step((0, "pe columns"), [(prep_v, "silu"), (w_in["wmod"], "in")], mod_columns, prep_t, "columns", columns)
        dve.step((0, "dve columns"), [(prep_t, "columns")],
                 lambda e: e.tensor_copy(sa_col[:, :], columns.ps[:, 0:BATCHES]), prep_v, "sa")
        dve.step((0, "dve columns"), [(prep_t, "columns")],
                 lambda e: e.tensor_scalar(ca_col[:, :], columns.ps[:, 4:4 + BATCHES], 1.0, None, ALU.add), prep_v, "ca")
        columns.read_by((prep_v, "ca"))
        batch_rows = Bank(turns)
        pe.step((0, "pe mod"), [(prep_v, "silu"), (w_in["wmod"], "in")], lambda e: e.matmul(
            batch_rows.ps[0:BATCHES, :], siluT[:, :], stage_m[:, 2 * P:6 * P], start=True, stop=True),
            prep_t, "rows", batch_rows)
        act.step((0, "act mod"), [(prep_t, "rows")], lambda e: e.activation(
            mod4.rearrange("b j n -> b (j n)"), batch_rows.ps[0:BATCHES, :], ACT.Copy), prep_a, "rows")
        batch_rows.read_by((prep_a, "rows"))
        gates = mod4[:, 0:4:3, :]
        dve.step((0, "dve mod"), [(prep_a, "rows")],
                 lambda e: e.tensor_scalar(mod4[:, 2, :], mod4[:, 2, :], 1.0, None, ALU.add), prep_v, "cb")
        dve.step((0, "dve mod"), [(prep_a, "rows")],
                 lambda e: e.tensor_scalar(sign4[:, :, :], gates, 0.0, 0.5, ALU.is_ge, ALU.subtract), prep_v, "sign")
        dve.step((0, "dve mod"), [(prep_a, "rows")],
                 lambda e: e.scalar_tensor_tensor(size4[:, :, :], gates, -1.0, gates, ALU.mult, ALU.max), prep_v, "size")
        dve.step((0, "dve mod"), [(prep_v, "sign"), (prep_v, "size")], lambda e: e.scalar_tensor_tensor(
            size4[:, :, :], size4[:, :, :], 0.25, sign4[:, :, :], ALU.max, ALU.mult), prep_v, "half")
        dve.step((0, "dve mod"), [(prep_v, "half")],
                 lambda e: e.tensor_scalar(gates, size4[:, :, :], 2.0, None, ALU.mult), prep_v, "gates")
        sp.step((0, "sp mod"), [(prep_v, "cb"), (prep_v, "gates")],
                lambda e: e.dma_start(mod_dram, mod4.rearrange("b j n -> b (j n)")), mod_out, "all")
        sp.step((0, "sp mod"), [(mod_out, "all")], lambda e: e.dma_start(
            mod[:, :, :, :].rearrange("p b j n -> p (b j n)"),
            mod_dram.rearrange("b n -> (b n)").unsqueeze(0).to_broadcast([P, BATCHES * 4 * P])), w_in["mod"], "in")

        def split(H, L, src, name, waits):
            act.step((0, "act " + name), waits, lambda e: e.activation(H, src, ACT.Copy), split_h, name)
            dve.step((0, "dve " + name), [(split_h, name)],
                     lambda e: e.tensor_tensor(L, src, H.bitcast(F32), ALU.subtract), split_l, name)

        split(WkH[:, :], WkL[:, :], stage_k, "wk", [(w_in["wk"], "in")])
        split(WvH[:, :], WvL[:, :], stage_v, "wv", [(w_in["wv"], "in")])
        for i in range(2):
            half = slice(i * HEADS * D // 2, (i + 1) * HEADS * D // 2)
            split(WqH[:, half], WqL[:, half], stage_q[:, half], f"wq{i}", [(w_in["wq"], "in")])
        for i in range(2):
            part = slice(i * REP, (i + 1) * REP)
            split(WoH[:, part, :], WoL[:, part, :], stage_o[:, part, :], f"wo{i}", [(w_in["wo"], (1, 1))])
        sp.step((0, "sp w1"), [(split_l, n) for n in ("wk", "wv", "wq0", "wq1", "wo0", "wo1")] + [(prep_t, n) for n in ("columns", "rows")],
                lambda e: e.dma_start(w1_sb, w1.rearrange("e h f -> h e f")), w_in["w1"], "in")

        def ln1(k):
            tiles = (2 * k, 2 * k + 1)
            for j, t in enumerate(tiles):
                dve.step((2 * k, f"dve stats1 {j}"),
                         [(x_in[t // BATCH_TILES], "in")] + ([(ln1_v, ("mv", t - 2))] if t >= 2 else []),
                         lambda e, t=t: e.bn_stats(stats1[:, t % 2, :], x_sb[:, t, :]), ln1_v, ("stats", t))
            for j, t in enumerate(tiles):
                dve.step((2 * k, f"dve mv1 {j}"), [(ln1_v, ("stats", t))],
                         lambda e, t=t: e.bn_aggr(mv1[:, t, :], stats1[:, t % 2, :]), ln1_v, ("mv", t))
            s = slice(2 * k, 2 * k + 2)
            pool.step((2 * k, "pool var1"), [(ln1_v, ("mv", t)) for t in tiles], lambda e: e.tensor_scalar(
                var1[:, s], mv1[:, s, 1], EPS, 1.0, ALU.add, ALU.mult), ln1_p, ("var", k))
            pool.step((2 * k, "pool rstd1"), [(ln1_p, ("var", k))], lambda e: e.tensor_tensor(
                rstd1[:, s], var1[:, s], neg_half[:, :], ALU.pow), ln1_p, ("rstd", k))
            for j, t in enumerate(tiles):
                dve.step((2 * k, f"dve norm1 {j}"), [(ln1_p, ("rstd", k))] + ([(x_turned, k - 1)] if k else []),
                         lambda e, t=t, j=j: e.tensor_scalar(
                             XN[:, j * P:(j + 1) * P], x_sb[:, t, :], mv1[:, t, 0:1], rstd1[:, t:t + 1],
                             ALU.subtract, ALU.mult), normed1, t)

        def turn_x(k):
            b = 2 * k // BATCH_TILES
            bank = Bank(turns)

            def turn(e):
                for j in range(2):
                    last = e.transpose(bank.ps[:, j * P:(j + 1) * P], XN[:, j * P:(j + 1) * P], ident[:, :])
                return last
            pe.step((2 * k, "pe x turn"), [(normed1, 2 * k), (normed1, 2 * k + 1), all_consts], turn, x_turned, k, bank)
            used = [(projected, (k - 2, n)) for n in ("v", "k", "q0", "q1", "q2", "q3")] if k >= 2 else []
            act.step((2 * k, "act xh"), [(x_turned, k), (prep_v, "sa"), (prep_v, "ca")] + used, lambda e: e.activation(
                XH[:, k % 2, :], bank.ps[:, 0:BT], ACT.Identity, bias=sa_col[:, b:b + 1], scale=ca_col[:, b:b + 1]),
                xh_done, k)
            dve.step((2 * k, "dve xf"), [(xh_done, k)] + ([(xl_done, k - 1)] if k else []), lambda e: e.tensor_scalar(
                XF[:, :], bank.ps[:, 0:BT], ca_col[:, b:b + 1], sa_col[:, b:b + 1], ALU.mult, ALU.add), xf_done, k)
            dve.step((2 * k, "dve xl"), [(xf_done, k)], lambda e: e.tensor_tensor(
                XL[:, k % 2, :], XF[:, :], XH[:, k % 2, :].bitcast(F32), ALU.subtract), xl_done, k)
            bank.read_by((xh_done, k), (xf_done, k))

        def three_passes(e, dst, wh, wl, xh, xl):
            e.matmul(dst, wh, xh, start=True, stop=False)
            e.matmul(dst, wh, xl, start=False, stop=False)
            return e.matmul(dst, wl, xh, start=False, stop=True)

        def project_k(k):
            bank = Bank(turns)

            def mm(e):
                for c in range(2):
                    w = slice(c * P, (c + 1) * P)
                    last = three_passes(e, bank.ps[:, c * BT:(c + 1) * BT], WkH[:, w], WkL[:, w],
                                        XH[:, k % 2, :], XL[:, k % 2, :])
                return last
            pe.step((2 * k, "pe k"), [(xl_done, k), (split_l, "wk")], mm, projected, (k, "k"), bank)
            used = [(scored, (2 * k - 4, h)) for h in range(2)] if k >= 3 else []
            halves = (slice(0, HALF), slice(HALF, P))
            for m in range(2):
                mine, other = halves[m], halves[1 - m]
                kh, kl = (t[:, k % K_RING, m::2, :] for t in (KH, KL))

                def source(mine=mine):
                    return bank.ps[mine, :].rearrange("p (c n) -> p c n", c=2)
                for half, name in ((mine, f"k {m}"), (other, f"k twice {m}")):
                    act.step((2 * k, "act " + name), [(projected, (k, "k"))] + used,
                             lambda e, kh=kh, half=half, source=source: e.activation(kh[half], source(), ACT.Copy),
                             h_kept, (k, name))
                    bank.read_by((h_kept, (k, name)))
                dve.step((2 * k, f"dve k {m}"), [(h_kept, (k, f"k {m}")), (h_kept, (k, f"k twice {m}"))],
                         lambda e, kh=kh, kl=kl, mine=mine, source=source: e.tensor_tensor(
                             kl[mine], source(), kh[mine].bitcast(F32), ALU.subtract), l_kept, (k, f"k {m}"))
                bank.read_by((l_kept, (k, f"k {m}")))
                dve.step((2 * k, f"dve k twice {m}"), [(l_kept, (k, f"k {m}"))],
                         lambda e, kl=kl, mine=mine, other=other: e.tensor_copy(kl[other], kl[mine].bitcast(F32)),
                         l_kept, (k, f"k twice {m}"))

        def project_v(k):
            bank = Bank(turns)

            def mm(e):
                for j in range(2):
                    tok = slice(j * P, (j + 1) * P)
                    dst = bank.ps[:, j * BT:(j + 1) * BT]
                    e.matmul(dst, XH[:, k % 2, tok], WvH[:, :], start=True, stop=False)
                    e.matmul(dst, XL[:, k % 2, tok], WvH[:, :], start=False, stop=False)
                    last = e.matmul(dst, XH[:, k % 2, tok], WvL[:, :], start=False, stop=True)
                return last
            pe.step((2 * k, "pe v"), [(xl_done, k), (split_l, "wv")], mm, projected, (k, "v"), bank)
            used = [(pv_done, (2 * k - 4, h)) for h in range(2)] if k >= 3 else []
            r = 2 * k % V_RING
            act.step((2 * k, "act v"), [(projected, (k, "v"))] + used, lambda e: e.activation(
                V[:, r:r + 2, :], bank.ps.rearrange("p (t n) -> p t n", t=2), ACT.Copy), v_kept, k)
            bank.read_by((v_kept, k))
            for j, t in enumerate((2 * k, 2 * k + 1)):
                if t % BATCH_TILES:
                    used = [(pv_done, (t - VD_RING, h)) for h in range(2)] if t >= VD_RING else []
                    pool.step((2 * k, f"pool vd {j}"), [(v_kept, k)] + used, lambda e, t=t: e.tensor_tensor(
                        VD[:, t % VD_RING, :], V[:, t % V_RING, :], V[:, (t - 1) % V_RING, :], ALU.subtract),
                        vd_done, t)

        def project_q(k, g):
            bank, name = Bank(turns), f"q{g}"

            def mm(e):
                for a in range(2):
                    w = slice((2 * g + a) * P, (2 * g + a + 1) * P)
                    last = three_passes(e, bank.ps[:, a * BT:(a + 1) * BT], WqH[:, w], WqL[:, w],
                                        XH[:, k % 2, :], XL[:, k % 2, :])
                return last
            pe.step((2 * k, "pe " + name), [(xl_done, k), (split_l, f"wq{g // 2}")], mm, projected, (k, name), bank)
            used = [(scored, (2 * k - 3, h)) for h in range(2)] if k >= 2 else []
            halves = (slice(0, HALF), slice(HALF, P))

            def head_pairs(half):
                return bank.ps[half, :].rearrange("p (c n) -> p c n", c=2)
            for odd in range(2):
                mine, other = halves[odd], halves[1 - odd]
                act.step((2 * k, f"act {name} {odd}"), [(projected, (k, name))] + used,
                         lambda e, odd=odd, mine=mine: e.activation(
                             T[mine, k % T_RING, 4 * g + odd:4 * g + 4:2, :], head_pairs(mine), ACT.Copy),
                         h_kept, (k, name, odd))
                dve.step((2 * k, f"dve {name} {odd}"), [(h_kept, (k, name, odd))],
                         lambda e, odd=odd, mine=mine, other=other: e.tensor_tensor(
                             T[other, k % T_RING, 4 * g + odd:4 * g + 4:2, :], head_pairs(mine),
                             T[mine, k % T_RING, 4 * g + odd:4 * g + 4:2, :].bitcast(F32), ALU.subtract),
                         l_kept, (k, name, odd))
                bank.read_by((l_kept, (k, name, odd)))

        def scores(t, h):
            k, first, u = t // 2, t % BATCH_TILES == 0, 2 * t + h
            last_unit = (t, 0) if h else (t - 1, 1)
            keys_ready = [(h_kept, (k, f"k twice {m}")) for m in range(2)] + [(l_kept, (k, f"k twice {m}")) for m in range(2)]

            def pair(e, dst, key_tile, g):
                q = T[:, k % T_RING, 4 * g:4 * g + 4, (t % 2) * P:(t % 2 + 1) * P]
                at = slice(key_tile % 2 * P, (key_tile % 2 + 1) * P)
                e.matmul(dst, KH[:, key_tile // 2 % K_RING, g, at], q, start=True, stop=False)
                return e.matmul(dst, KL[:, key_tile // 2 % K_RING, g, at], q, start=False, stop=True)

            for a in range(2):
                g = 2 * h + a
                pe.step((t, f"pe own {h}"), keys_ready + [(l_kept, (k, f"q{g}", 0)), (l_kept, (k, f"q{g}", 1))]
                        + ([(tanhed, last_unit)] if u else []),
                        lambda e, a=a, g=g: pair(e, own[:, a, :], t, g), scored, (t, h) if first and a else (t, h, "own", a))
            if not first:
                for a in range(2):
                    g = 2 * h + a
                    bank = Bank(turns)
                    pe.step((t, f"pe before {h}"), [(l_kept, (k, f"q{g}", 0)), (l_kept, (k, f"q{g}", 1))],
                            lambda e, g=g, bank=bank: pair(e, bank.ps, t - 1, g),
                            scored, (t, h) if a else (t, h, "before"), bank)
                    dve.step((t, f"dve merge {h} {a}"), [(scored, (t, h, "own", a)), (scored, (t, h) if a else (t, h, "before"))],
                             lambda e, a=a, bank=bank: e.copy_predicated(
                                 own[:, a, :].rearrange("p (r n) -> p r n", n=P),
                                 before[:, :].bitcast(U32).unsqueeze(1).to_broadcast([P, REP, P]),
                                 bank.ps.rearrange("p (r n) -> p r n", n=P)), merged, (t, h, a))
                    bank.read_by((merged, (t, h, a)))
            source = [(scored, (t, h))] if first else [(merged, (t, h, 0)), (merged, (t, h, 1))]
            pr, pm = PR[:, u % P_RING, :], PM[:, u % PM_RING, :]
            used = [(summed, t - 2), (pv_done, (t - 2, h)), (masked, (t - 2, h))] if t >= 2 else []
            act.step((t, f"act tanh {h}"), source + used, lambda e: e.activation(
                pr, own[:, :, :].rearrange("p a n -> p (a n)"), ACT.Tanh, scale=SCORE_SCALE), tanhed, (t, h))
            act.step((t, f"act exp {h}"), [(tanhed, (t, h))],
                     lambda e: e.activation(pr, pr, ACT.Exp, scale=SOFTCAP), exped, (t, h))
            used = []
            if u >= PM_RING:
                ot, oh = divmod(u - PM_RING, 2)
                used.append((pv_done, (ot, oh)))
                if ot % BATCH_TILES == 0:
                    used.append((summed, ot))
            pool.step((t, f"pool mask {h}"), [(exped, (t, h))] + used, lambda e: e.affine_select(
                out=pm.rearrange("p (r n) -> p r n", n=P), in_=pr.rearrange("p (r n) -> p r n", n=P),
                compare_op=ALU.is_ge, fill=0.0, base=0, pattern=[[0, 2 * REP], [1, P]], channel_multiplier=-1),
                masked, (t, h))

        def attend(t, h):
            first, u = t % BATCH_TILES == 0, 2 * t + h
            bank = Bank(turns)

            def mm(e):
                parts = [(V, PM, u % PM_RING, t % V_RING)] if first else [
                    (V, PR, u % P_RING, (t - 1) % V_RING), (VD, PM, u % PM_RING, t % VD_RING)]
                for m, (v, p, pr, vr) in enumerate(parts):
                    for a in range(2):
                        g = 2 * h + a
                        last = e.matmul(bank.ps[a * HALF:(a + 1) * HALF, :], v[:, vr, g * D:(g + 1) * D],
                                        p[:, pr, a * REP * P:(a + 1) * REP * P],
                                        start=(m == 0), stop=(m == len(parts) - 1))
                return last
            ready = [(masked, (t, h)), (v_kept, t // 2)] + ([] if first else [(vd_done, t)])
            pe.step((t, f"pe pv {h}"), ready, mm, pv_done, (t, h), bank)
            used = [(oh_done, (t - 2, h)), (ol_done, (t - 2, h))] if t >= 2 else []
            act.step((t, f"act ou {h}"), [(pv_done, (t, h))] + used,
                     lambda e: e.activation(OU[:, u % 4, :], bank.ps, ACT.Copy), o_kept, (t, h))
            bank.read_by((o_kept, (t, h)))

        def sums(t):
            first = t % BATCH_TILES == 0
            bank = Bank(turns)

            def mm(e):
                for g in range(KV):
                    u = 2 * t + g // 2
                    p = PM[:, u % PM_RING, :] if first else PR[:, u % P_RING, :]
                    last = e.matmul(bank.ps[32 * g:32 * g + 32, :], ones32[:, :],
                                    p[:, (g % 2) * REP * P:(g % 2 + 1) * REP * P], start=True, stop=True,
                                    tile_position=(0, 32 * g))
                return last
            pe.step((t, "pe sums"), [(masked if first else exped, (t, h)) for h in range(2)], mm, summed, t, bank)
            act.step((t, "act sums"), [(summed, t)] + ([(sums_turned, t - 1)] if t else []),
                     lambda e: e.activation(SUMS[:, :], bank.ps, ACT.Copy), sums_kept, t)
            bank.read_by((sums_kept, t))

        def invert(t):
            bank = Bank(turns)

            def turn(e):
                for r in range(REP):
                    last = e.transpose(bank.ps[:, r * P:(r + 1) * P], SUMS[:, r * P:(r + 1) * P], ident[:, :])
                return last
            pe.step((t, "pe sums turn"), [(sums_kept, t)], turn, sums_turned, t, bank)
            dve.step((t, "dve invert"), [(sums_turned, t)] + ([(repeated, t - 1)] if t else []), lambda e: e.reciprocal(
                RS[:, :].rearrange("q (p r h) -> q r p h", p=2, r=REP),
                bank.ps[:, 0:REP * P:32].rearrange("q (r p h) -> q r p h", r=REP, p=2)), inverted, t)
            bank.read_by((inverted, t))
            pool.step((t, "pool repeat"), [(inverted, t)] + ([(rs_turned, (t - 1, h)) for h in range(2)] if t else [(mod_out, "all")]),
                      lambda e: e.tensor_scalar(
                          RX[:, :, :], RS[:, :].unsqueeze(2).to_broadcast([P, HEADS, D]), 1.0, 1.0, ALU.mult, ALU.mult),
                      repeated, t)

        def scale(t, h):
            bank = Bank(turns)

            def turn(e):
                for r in range(REP):
                    i = 2 * (h * REP + r)
                    last = e.transpose(bank.ps[:, r * P:(r + 1) * P], RX[:, i:i + 2, :].rearrange("q a d -> q (a d)"),
                                       ident[:, :])
                return last
            pe.step((t, f"pe rs turn {h}"), [(repeated, t)], turn, rs_turned, (t, h), bank)
            o = OU[:, (2 * t + h) % 4, :]
            dve.step((t, f"dve scale {h}"), [(rs_turned, (t, h)), (o_kept, (t, h))],
                     lambda e: e.tensor_tensor(o, bank.ps, o, ALU.mult), scaled, (t, h))
            bank.read_by((scaled, (t, h)))
            used = [(wo_done, t // 2 - 1)] if t >= 2 else []
            oh, ol = OH[:, t % 2, h, :], OL[:, t % 2, h, :]
            act.step((t, f"act oh {h}"), [(scaled, (t, h))] + used, lambda e: e.activation(oh, o, ACT.Copy),
                     oh_done, (t, h))
            pool.step((t, f"pool ol {h}"), [(oh_done, (t, h))],
                      lambda e: e.tensor_tensor(ol, o, oh.bitcast(F32), ALU.subtract), ol_done, (t, h))

        def out_project(k):
            bank = Bank(turns)

            def mm(e):
                y = bank.ps[:, 0:BT]
                for i in range(2 * REP):
                    h, r = divmod(i, REP)
                    oh, ol = (o[:, :, h, r * P:(r + 1) * P] for o in (OH, OL))
                    e.matmul(y, WoH[:, i, :], oh, start=(i == 0), stop=False)
                    e.matmul(y, WoH[:, i, :], ol, start=False, stop=False)
                    last = e.matmul(y, WoL[:, i, :], oh, start=False, stop=(i == 2 * REP - 1))
                return last
            both = [(ol_done, (t, h)) for t in (2 * k, 2 * k + 1) for h in range(2)]
            pe.step((2 * k, "pe wo"), both + [(split_l, "wo0"), (split_l, "wo1")], mm, wo_done, k, bank)
            used = [(y_turned, t) for t in (2 * k - 2, 2 * k - 1)] if k else [all_consts]
            act.step((2 * k, "act y"), [(wo_done, k)] + used,
                     lambda e: e.activation(YT[:, :], bank.ps[:, 0:BT], ACT.Copy), yT_kept, k)
            bank.read_by((yT_kept, k))

        def residual(t):
            b = t // BATCH_TILES
            bank = Bank(turns)
            pe.step((t, "pe y turn"), [(yT_kept, t // 2)], lambda e: e.transpose(
                bank.ps[:, 0:P], YT[:, t % 2 * P:(t % 2 + 1) * P], ident[:, :]), y_turned, t, bank)
            r = t % PAY_RING
            xr = PAY[:, r, ROW_X:ROW_X + P]
            used = [(pay_out[r], t - PAY_RING), (x1_out[r], t - PAY_RING)] if t >= PAY_RING else [(empty_in, "all")]
            dve.step((t, "dve ga"), [(y_turned, t), (w_in["mod"], "in")] + used, lambda e: e.tensor_tensor(
                xr, bank.ps[:, 0:P], mod[:, b, 0, :], ALU.mult), tail_v, ("ga", t))
            bank.read_by((tail_v, ("ga", t)))
            dve.step((t, "dve x1"), [(tail_v, ("ga", t))], lambda e: e.tensor_tensor(xr, xr, x_sb[:, t, :], ALU.add),
                     tail_v, ("x1", t))
            sp.step((t, "sp x1"), [(tail_v, ("x1", t))],
                    lambda e: e.dma_start(out[t * P:(t + 1) * P, :], xr), x1_out[r], t)
            dve.step((t, "dve stats2"), [(tail_v, ("x1", t))] + ([(tail_v, ("mv", t - 1))] if t else []),
                     lambda e: e.bn_stats(stats2[:, :], xr), tail_v, ("stats", t))
            dve.step((t, "dve mv2"), [(tail_v, ("stats", t))],
                     lambda e: e.bn_aggr(mv2[:, t, :], stats2[:, :]), tail_v, ("mv", t))
            pool.step((t, "pool var2"), [(tail_v, ("mv", t))], lambda e: e.tensor_scalar(
                var2[:, t:t + 1], mv2[:, t, 1:2], EPS, 1.0, ALU.add, ALU.mult), ln2_p, ("var", t))
            pool.step((t, "pool rstd2"), [(ln2_p, ("var", t))], lambda e: e.tensor_tensor(
                rstd2[:, t:t + 1], var2[:, t:t + 1], neg_half[:, 0:1], ALU.pow), ln2_p, ("rstd", t))

        def normalise2(t):
            b = t // BATCH_TILES
            pay = PAY[:, t % PAY_RING, :]
            xr, hr = pay[:, ROW_X:ROW_X + P], pay[:, ROW_H:ROW_H + P]
            dve.step((t, "dve n"), [(ln2_p, ("rstd", t))], lambda e: e.tensor_scalar(
                hr, xr, mv2[:, t, 0:1], rstd2[:, t:t + 1], ALU.subtract, ALU.mult), tail_v, ("n", t))
            dve.step((t, "dve m"), [(tail_v, ("n", t))],
                     lambda e: e.tensor_tensor(hr, hr, mod[:, b, 2, :], ALU.mult), tail_v, ("m", t))
            dve.step((t, "dve h2"), [(tail_v, ("m", t))],
                     lambda e: e.tensor_tensor(hr, hr, mod[:, b, 1, :], ALU.add), tail_v, ("h2", t))
            bank = Bank(turns)
            pe.step((t, "pe h2 turn"), [(tail_v, ("h2", t))], lambda e: e.transpose(bank.ps[:, 0:P], hr, ident[:, :]),
                    h2_turned, t, bank)
            act.step((t, "act h2"), [(h2_turned, t)] + ([(logits_done, t - 1)] if t else []),
                     lambda e: e.activation(h2T[:, :], bank.ps[:, 0:P], ACT.Copy), h2_kept, t)
            bank.read_by((h2_kept, t))

        def route(t):
            b = t // BATCH_TILES
            bank = Bank(turns)
            pe.step((t, "pe logits"), [(h2_kept, t), (w_in["rest"], 1)], lambda e: e.matmul(
                bank.ps[:, 0:EXPERTS], h2T[:, :], Wg[:, :], start=True, stop=True), logits_done, t, bank)
            lg = logits[:, t, :]
            dve.step((t, "dve l"), [(logits_done, t)], lambda e: e.tensor_copy(lg, bank.ps[:, 0:EXPERTS]),
                     route_v, ("l", t))
            bank.read_by((route_v, ("l", t)))
            dve.step((t, "dve top"), [(route_v, ("l", t))], lambda e: e.max(top[:, t, :], lg), route_v, ("top", t))
            dve.step((t, "dve at"), [(route_v, ("top", t))], lambda e: e.max_index(top_at[:, t, :], top[:, t, :], lg),
                     route_v, ("at", t))
            dve.step((t, "dve neg"), [(route_v, ("top", t))], lambda e: e.tensor_scalar(
                neg_top[:, t:t + 1], top[:, t, 0:1], -1.0, None, ALU.mult), route_v, ("neg", t))
            dve.step((t, "dve one"), [(route_v, ("at", t))], lambda e: e.tensor_scalar(
                onehot[:, t, :], iota8[:, :], top_at[:, t, 0:1], None, ALU.is_equal), route_v, ("one", t))
            dve.step((t, "dve seen"), [(route_v, ("one", t))] + ([(route_v, ("seen", t - 1))] if t else []),
                     lambda e: e.tensor_tensor(seen[:, t + 1, :], seen[:, t, :], onehot[:, t, :], ALU.add),
                     route_v, ("seen", t))
            act.step((t, "act gate"), [(route_v, ("neg", t))] + ([(gate_e, t - 1)] if t else []), lambda e: e.activation(
                e8[:, :], lg, ACT.Exp, bias=neg_top[:, t:t + 1], accum_out=e_sum[:, t:t + 1]), gate_e, t)
            dve.step((t, "dve gate"), [(gate_e, t)], lambda e: e.reciprocal(gate[:, t:t + 1], e_sum[:, t:t + 1]),
                     route_v, ("gate", t))
            dve.step((t, "dve g"), [(route_v, ("gate", t))], lambda e: e.tensor_scalar(
                PAY[:, t % PAY_RING, ROW_G:ROW_G + P], mod[:, b, 3, :], gate[:, t:t + 1], None, ALU.mult),
                route_v, ("g", t))

        def place(t):
            bank = Bank(turns)

            def mm(e):
                e.matmul(bank.ps[:, 0:EXPERTS], earlier_b[:, :], onehot[:, t, :], start=True, stop=False)
                return e.matmul(bank.ps[:, 0:EXPERTS], ones_b[:, :], seen[:, t, :], start=False, stop=True)
            pe.step((t, "pe count"), [(route_v, ("one", t))] + ([(route_v, ("seen", t - 1))] if t else []),
                    mm, placed, t, bank)
            one = slice(t, t + 1)
            dve.step((t, "dve loc"), [(placed, t)] + ([(route_v, ("loc", t - 1))] if t else []),
                     lambda e: e.tensor_tensor_reduce(
                out=prod8[:, :], in0=bank.ps[:, 0:EXPERTS], in1=onehot[:, t, :], scale=1.0, scalar=0.0,
                op0=ALU.mult, op1=ALU.add, accum_out=loc[:, one]), route_v, ("loc", t))
            bank.read_by((route_v, ("loc", t)))
            dve.step((t, "dve slot"), [(route_v, ("loc", t))], lambda e: e.scalar_tensor_tensor(
                slot[:, one], top_at[:, t, 0:1], float(CAP), loc[:, one], ALU.mult, ALU.add), route_v, ("slot", t))
            dve.step((t, "dve over"), [(route_v, ("loc", t))], lambda e: e.tensor_scalar(
                over[:, one], loc[:, one], float(CAP), float(2 * TOKENS), ALU.is_ge, ALU.mult), route_v, ("over", t))
            dve.step((t, "dve slot_i"), [(route_v, ("over", t)), (route_v, ("slot", t))], lambda e: e.tensor_tensor(
                slot_i[:, one], slot[:, one], over[:, one], ALU.add), route_v, ("slot_i", t))
            r = t % PAY_RING
            used = [(pay_out[r], t - PAY_RING)] if t >= PAY_RING else [(empty_in, "all")]
            pool.step((t, "pool id"), used, lambda e: e.tensor_copy(
                PAY[:, r, ROW_ID:ROW_ID + 1].bitcast(I32), tok_id[:, one]), payload_p, t)
            waits = [(payload_p, t), (route_v, ("slot_i", t)), (route_v, ("g", t)), (empty_in, "all")]
            pool.step((t, "pool scatter"), waits, lambda e: e.indirect_dma_start(
                sorted_rows, bass.IndirectOffsetOnAxis(ap=slot_i[:, one], axis=0), PAY[:, r, :], None,
                bounds_check=TOKENS - 1, oob_is_err=False), pay_out[r], t)

        for k in range(BLOCKS):
            ln1(k)
            turn_x(k)
            project_k(k)
            project_v(k)
            for g in range(KV):
                project_q(k, g)
        for t in range(TILES):
            for h in range(2):
                scores(t, h)
                attend(t, h)
            sums(t)
            invert(t)
            for h in range(2):
                scale(t, h)
            if t % 2:
                out_project(t // 2)
            residual(t)
            normalise2(t)
            route(t)
            place(t)
        for queue in engines:
            queue.order()
            queue.part += 1
        held = place_banks(pe)

        turn_banks = [turns[:, n, :] for n in (0, 1)]
        up_banks = [own[:, 0, :], own[:, 1, :], turns[:, 2, :], turns[:, 3, :]]
        down_banks = [turns[:, n, :] for n in (4, 5)]
        sorted_v = sorted_rows.rearrange("(e s p) r -> e p s r", s=ST, p=P)

        every_row = [(pay_out[t % PAY_RING], t) for t in range(TILES - PAY_RING, TILES)] + [(empty_in, "all")]
        every_row += [(tail_v, ("x1", TILES - 1)), (scored, (TILES - 1, 0)), (scored, (TILES - 1, 1))]

        def load_rows(e_):
            parts = [(slice(0, P), rows_in[0]), (slice(P, ROW), rest_in)] if e_ == 0 else [(slice(0, ROW), rows_in[e_])]
            for part, arrived in parts:
                sp.step(None, every_row, lambda e, part=part: e.dma_start(rows[e_][:, :, part], sorted_v[e_][:, :, part]),
                        arrived, "in")
            sp.step(None, [(s, (t, h)) for s in (pv_done, oh_done, ol_done) for t in (TILES - 2, TILES - 1)
                           for h in range(2)], lambda e: e.dma_start(
                W2[e_ // (EXPERTS // 2)][:, e_ % (EXPERTS // 2) * FC:(e_ % (EXPERTS // 2) + 1) * FC, :], w2[e_].rearrange("(c p) n -> p c n", p=P)), w2_in[e_], "in")

        def split_w1(e_):
            used = [(up_done, (e_ - 2, FC - 1))] if e_ >= 2 else [(projected, (BLOCKS - 1, f"q{g}")) for g in range(KV)]
            act.step(None, [(w_in["w1"], "in")] + used,
                     lambda e: e.activation(w1H[:, e_ % 2, :], w1_sb[:, e_, :], ACT.Copy), w1H_kept, e_)
            dve.step(None, [(w1H_kept, e_)], lambda e: e.tensor_tensor(
                w1L[:, e_ % 2, :], w1_sb[:, e_, :], w1H[:, e_ % 2, :].bitcast(F32), ALU.subtract), w1L_kept, e_)

        def turn_rows(e_):
            ps = turn_banks[e_ % 2]

            def turn(e):
                for s in range(ST):
                    last = e.transpose(ps[:, s * P:(s + 1) * P], rows[e_][:, s, ROW_H:ROW_H + P], ident[:, :])
                return last
            free = [(xTL_kept, e_ - 2)] if e_ >= 2 else held[e_].readers
            pe.step(None, [(rows_in[e_], "in")] + free, turn, rows_turned, e_)
            used = [(up_done, (e_ - 2, FC - 1))] if e_ >= 2 else [(scored, (TILES - 1, h)) for h in range(2)]
            act.step(None, [(rows_turned, e_)] + used, lambda e: e.activation(xTH[:, e_ % 2, :], ps, ACT.Copy),
                     xTH_kept, e_)
            dve.step(None, [(xTH_kept, e_)], lambda e: e.tensor_tensor(
                xTL[:, e_ % 2, :], ps, xTH[:, e_ % 2, :].bitcast(F32), ALU.subtract), xTL_kept, e_)

        def up(e_):
            n = e_ % 2
            for f in range(FC):
                w = slice(f * P, (f + 1) * P)
                free = [(relu_done, (e_ - 1, f))] if e_ else [(tanhed, (TILES - 1, 1))] + held[f].readers
                pe.step(None, [(xTL_kept, e_), (w1L_kept, e_)] + free, lambda e, f=f, w=w: three_passes(
                    e, up_banks[f], w1H[:, n, w], w1L[:, n, w], xTH[:, n, :], xTL[:, n, :]), up_done, (e_, f))
                used = [(down_done, (e_ - 2, 1))] if e_ >= 2 else [
                    (summed, TILES - 1), (pv_done, (TILES - 1, 0)), (pv_done, (TILES - 1, 1)),
                    (masked, (TILES - 1, 0)), (masked, (TILES - 1, 1))]
                act.step(None, [(up_done, (e_, f)), (w_in["rest"], 1)] + used, lambda e, f=f: e.activation(
                    hidden[n][:, f, :], up_banks[f], ACT.Relu, bias=b1_col[:, e_, f:f + 1]), relu_done, (e_, f))

        def down(e_):
            for pair in range(2):
                ps = down_banks[pair]
                tiles = slice(2 * pair, 2 * pair + 2)

                def mm(e, ps=ps, pair=pair):
                    for s in (2 * pair, 2 * pair + 1):
                        for f in range(FC):
                            last = e.matmul(ps[:, s % 2 * P:(s % 2 + 1) * P], hidden[e_ % 2][:, f, s * P:(s + 1) * P],
                                            W2[e_ // (EXPERTS // 2)][:, e_ % (EXPERTS // 2) * FC + f, :], start=(f == 0), stop=(f == FC - 1))
                    return last
                free = [(out_v, (e_ - 1, "b2", pair))] if e_ else held[4 + pair].readers
                pe.step(None, [(relu_done, (e_, FC - 1)), (w2_in[e_], "in")] + free, mm, down_done, (e_, pair))
                dst, rw = done_rows[e_ % 2][:, tiles, :], rows[e_][:, tiles, :]
                used = [(final_out[e_ % 2], (e_ - 2, ST - 1))] if e_ >= 2 else [(pv_done, (TILES - 1, 0)), (pv_done, (TILES - 1, 1))]
                bank = ps[:, 0:2 * P].rearrange("p (s d) -> p s d", s=2)
                dve.step(None, [(down_done, (e_, pair)), (w_in["b2"], "in")] + used, lambda e, dst=dst, bank=bank: e.tensor_tensor(
                    dst, bank, b2_row[:, e_, :].unsqueeze(1).to_broadcast([P, 2, P]), ALU.add), out_v, (e_, "b2", pair))
                dve.step(None, [(out_v, (e_, "b2", pair)), (rows_in[e_] if e_ else rest_in, "in")], lambda e, dst=dst, rw=rw: e.tensor_tensor(
                    dst, dst, rw[:, :, ROW_G:ROW_G + P], ALU.mult), out_v, (e_, "g", pair))
                dve.step(None, [(out_v, (e_, "g", pair))], lambda e, dst=dst, rw=rw: e.tensor_tensor(
                    dst, dst, rw[:, :, ROW_X:ROW_X + P], ALU.add), out_v, (e_, "x", pair))
                for s in range(2):
                    waits = [(out_v, (e_, "x", pair))] + [(x1_out[t % PAY_RING], t) for t in range(TILES - PAY_RING, TILES)]
                    pool.step(None, waits, lambda e, s=s, dst=dst, rw=rw: e.indirect_dma_start(
                        out, bass.IndirectOffsetOnAxis(ap=rw[:, s, ROW_ID:ROW_ID + 1].bitcast(I32), axis=0),
                        dst[:, s, :], None, bounds_check=TOKENS - 1, oob_is_err=False),
                        final_out[e_ % 2], (e_, 2 * pair + s))

        sp.step(None, [(pv_done, (TILES - 1, 0)), (pv_done, (TILES - 1, 1))], lambda e: e.dma_start(
            b2_row, b2.unsqueeze(0).to_broadcast([P, EXPERTS, P])), w_in["b2"], "in")
        for e_ in range(EXPERTS):
            load_rows(e_)
        split_w1(0)
        split_w1(1)
        turn_rows(0)
        up(0)
        turn_rows(1)
        for e_ in range(1, EXPERTS - 1):
            up(e_)
            split_w1(e_ + 1)
            turn_rows(e_ + 1)
            down(e_ - 1)
        down(EXPERTS - 2)
        up(EXPERTS - 1)
        down(EXPERTS - 1)
        sp.step(None, [(final_out[n], (EXPERTS - 2 + n, ST - 1)) for n in range(2)], lambda e: None)
        for queue in engines:
            queue.count()

        block = ctx.enter_context(nc.Block())
        block.sync(sp.run)
        block.tensor(pe.run)
        block.scalar(act.run)
        block.vector(dve.run)
        block.gpsimd(pool.run)


def kernel(L0_attn_x, L0_attn_Wq, L0_attn_Wk, L0_attn_Wv, L0_attn_Wo, L0_ffn_Wg, L0_ffn_W1, L0_ffn_b1,
           L0_ffn_W2, L0_ffn_b2, L0_c, L0_wmod):
    import concourse.bacc as bacc
    from concourse.bass_utils import run_bass_kernel_spmd

    ascon = np.ascontiguousarray
    arrays = {
        "x": ascon(L0_attn_x).reshape(TOKENS, P),
        "wq": ascon(np.transpose(L0_attn_Wq)),
        "wk": ascon(np.transpose(L0_attn_Wk)),
        "wv": ascon(np.transpose(L0_attn_Wv)),
        "wo": ascon(np.transpose(L0_attn_Wo)),
        "wg": ascon(L0_ffn_Wg),
        "w1": ascon(L0_ffn_W1),
        "b1": ascon(np.transpose(np.reshape(L0_ffn_b1, (EXPERTS, FC, P)), (2, 0, 1))),
        "w2": ascon(L0_ffn_W2),
        "b2": ascon(L0_ffn_b2),
        "c": ascon(np.transpose(L0_c)),
        "wmod": ascon(L0_wmod),
    }
    nc = bacc.Bacc("TRN2", target_bir_lowering=False, num_devices=1)
    args = [nc.dram_tensor(f"{n}_dram", a.shape, F32, kind="ExternalInput").ap() for n, a in arrays.items()]
    out = nc.dram_tensor("out_dram", (TOKENS, P), F32, kind="ExternalOutput").ap()
    build(nc, *args, out)
    r = run_bass_kernel_spmd(nc, [{f"{n}_dram": a for n, a in arrays.items()}], core_ids=[0])
    return r.results[0]["out_dram"].reshape(BATCHES, SEQ, P)
```
